# Optimizing a Trainium2 kernel written in Bass

```python
import numpy as np
import jax
import jax.numpy as jnp

def _softmax(x, axis=-1):
    return jax.nn.softmax(x, axis=axis)

def _gelu(x):
    return jax.nn.gelu(x, approximate=True)

def _silu(x):
    return jax.nn.silu(x)

def _sigmoid(x):
    return jax.nn.sigmoid(x)

def _layernorm(x, axis=-1, eps=1e-05):
    m = jnp.mean(x, axis=axis, keepdims=True)
    v = jnp.var(x, axis=axis, keepdims=True)
    return (x - m) / jnp.sqrt(v + eps)

def _scatter_add(tgt, idx, src, axis=0):
    return tgt.at[idx].add(src)

def _segment_sum(src, seg, n):
    return jax.ops.segment_sum(src, seg, n)
kernel_name = 'mk_xattn_seq_d2_seqx_r4_5b17e3'

def setup_inputs(seed: int=0):
    np.random.seed(seed)
    _w = jnp.asarray

    def _rec_inputs():
        import jax
        import jax.numpy as jnp
        _rk = jax.random.key(seed)
        x = -0.0003929 + 0.9999 * jax.random.normal(jax.random.fold_in(_rk, 1), (16, 256, 512), jnp.float32)
        _lenS = 256 - jax.random.randint(jax.random.fold_in(_rk, 7), (16,), 0, max(1, 256 // 4) + 1, jnp.int32)
        _lenS2 = 256 - jax.random.randint(jax.random.fold_in(_rk, 8), (16,), 0, max(1, 256 // 4) + 1, jnp.int32)
        _ctx_2048P = jax.random.normal(jax.random.fold_in(_rk, 11), (16, 16, 512), jnp.float32)
        _ctx_2048c = jax.random.dirichlet(jax.random.fold_in(_rk, 511), 0.3 * jnp.ones((16,), jnp.float32), (16, 256))
        _ctx_2048t = jnp.einsum('bsk,bkd->bsd', _ctx_2048c, _ctx_2048P)
        _ctx_2048t = _ctx_2048t * jax.lax.rsqrt(jnp.mean(jnp.square(_ctx_2048t)) + 1e-12) * 0.953939
        ctx_2048 = 2.81802e-05 + 1.00001 * (_ctx_2048t + 0.3 * jax.random.normal(jax.random.fold_in(_rk, 611), (16, 256, 512), jnp.float32))
        _validS = jnp.arange(256)[None, :] < _lenS[:, None]
        _validS2 = jnp.arange(256)[None, :] < _lenS2[:, None]
        _causal = jnp.tril(jnp.ones((256, 256), dtype=bool))
        mask_BxS2_ik0 = jnp.where(jnp.broadcast_to(_validS2[:, :], (16, 256)), 0, 1).astype(jnp.int32)
        return (x, ctx_2048, mask_BxS2_ik0)
    x, ctx_2048, mask_BxS2_ik0 = _rec_inputs()

    def _L0_xattn_setup():
        import jax, jax.numpy as jnp
        import numpy as np
        B, C1, C2, N = (8, 256, 256, 512)
        D = C2 // 8
        key = jax.random.key(seed)
        ks = jax.random.split(key, 8)
        s1 = 1.0 / np.sqrt(C1)
        s2 = 1.0 / np.sqrt(C2)
        return {'x1': jax.random.normal(ks[0], (B, C1, N), jnp.float32), 'x2': jax.random.normal(ks[1], (B, C2, N), jnp.float32), 'Wq': jax.random.uniform(ks[2], (D, C1), jnp.float32, -s1, s1), 'bq': jax.random.uniform(ks[3], (D,), jnp.float32, -s1, s1), 'Wk': jax.random.uniform(ks[4], (D, C2), jnp.float32, -s2, s2), 'bk': jax.random.uniform(ks[5], (D,), jnp.float32, -s2, s2), 'Wv': jax.random.uniform(ks[6], (C1, C2), jnp.float32, -s2, s2), 'bv': jax.random.uniform(ks[7], (C1,), jnp.float32, -s2, s2)}
    _L0_xattn_all = _L0_xattn_setup()
    _L0_xattn_in = {k: v for k, v in _L0_xattn_all.items() if k in ('Wq', 'bq', 'Wk', 'bk', 'Wv', 'bv')}
    del _L0_xattn_all

    def _L1_xattn_setup():
        import jax, jax.numpy as jnp
        import numpy as np
        B, P, K, H, NH = (4, 512, 64, 512, 16)
        DH = H // NH
        EPS = 1e-06

        def rmsnorm(x, w):
            var = jnp.mean(jnp.square(x), axis=-1, keepdims=True)
            return x * jax.lax.rsqrt(var + EPS) * w
        key = jax.random.key(seed)
        ks = jax.random.split(key, 12)
        s = 0.02
        return {'x': jax.random.normal(ks[0], (B, P, H), jnp.float32), 'latents': jax.random.normal(ks[1], (B, K, H), jnp.float32), 'attention_mask': jax.random.randint(ks[2], (B, P), 0, 2, jnp.int32), 'q_w': s * jax.random.normal(ks[3], (H, H), jnp.float32), 'q_b': jnp.zeros((H,), jnp.float32), 'kv_w': s * jax.random.normal(ks[4], (H, 2 * H), jnp.float32), 'kv_b': jnp.zeros((2 * H,), jnp.float32), 'out_w': s * jax.random.normal(ks[5], (H, H), jnp.float32), 'out_b': jnp.zeros((H,), jnp.float32), 'postnorm_w': jnp.ones((H,), jnp.float32), 'mlp_w1': s * jax.random.normal(ks[6], (H, 4 * H), jnp.float32), 'mlp_b1': jnp.zeros((4 * H,), jnp.float32), 'mlp_w2': s * jax.random.normal(ks[7], (4 * H, H), jnp.float32), 'mlp_b2': jnp.zeros((H,), jnp.float32)}
    _L1_xattn_all = _L1_xattn_setup()
    _L1_xattn_in = {k: v for k, v in _L1_xattn_all.items() if k in ('q_w', 'q_b', 'kv_w', 'kv_b', 'out_w', 'out_b', 'postnorm_w', 'mlp_w1', 'mlp_b1', 'mlp_w2', 'mlp_b2')}
    del _L1_xattn_all
    return {'x': x, 'ctx_2048': ctx_2048, 'mask_BxS2_ik0': mask_BxS2_ik0, 'L0_xattn_Wq': _L0_xattn_in['Wq'], 'L0_xattn_bq': _L0_xattn_in['bq'], 'L0_xattn_Wk': _L0_xattn_in['Wk'], 'L0_xattn_bk': _L0_xattn_in['bk'], 'L0_xattn_Wv': _L0_xattn_in['Wv'], 'L0_xattn_bv': _L0_xattn_in['bv'], 'L1_xattn_q_w': _L1_xattn_in['q_w'], 'L1_xattn_q_b': _L1_xattn_in['q_b'], 'L1_xattn_kv_w': _L1_xattn_in['kv_w'], 'L1_xattn_kv_b': _L1_xattn_in['kv_b'], 'L1_xattn_out_w': _L1_xattn_in['out_w'], 'L1_xattn_out_b': _L1_xattn_in['out_b'], 'L1_xattn_postnorm_w': _L1_xattn_in['postnorm_w'], 'L1_xattn_mlp_w1': _L1_xattn_in['mlp_w1'], 'L1_xattn_mlp_b1': _L1_xattn_in['mlp_b1'], 'L1_xattn_mlp_w2': _L1_xattn_in['mlp_w2'], 'L1_xattn_mlp_b2': _L1_xattn_in['mlp_b2']}

def reference(x, ctx_2048, mask_BxS2_ik0, L0_xattn_Wq, L0_xattn_bq, L0_xattn_Wk, L0_xattn_bk, L0_xattn_Wv, L0_xattn_bv, L1_xattn_q_w, L1_xattn_q_b, L1_xattn_kv_w, L1_xattn_kv_b, L1_xattn_out_w, L1_xattn_out_b, L1_xattn_postnorm_w, L1_xattn_mlp_w1, L1_xattn_mlp_b1, L1_xattn_mlp_w2, L1_xattn_mlp_b2):
    import jax
    import jax.numpy as jnp

    def _L0_xattn_ref(x1, x2, Wq, bq, Wk, bk, Wv, bv):
        import jax, jax.numpy as jnp
        import numpy as np
        B, C1, C2, N = (8, 256, 256, 512)
        D = C2 // 8
        q = jnp.einsum('bcn,dc->bnd', x1, Wq) + bq
        k = jnp.einsum('bcn,dc->bdn', x2, Wk) + bk[:, None]
        v = jnp.einsum('bcn,dc->bdn', x2, Wv) + bv[:, None]
        attn = jax.nn.softmax(jnp.einsum('bnd,bdm->bnm', q, k), axis=2)
        attn_out = jnp.einsum('bcm,bnm->bcn', v, attn)
        return attn_out + x1

    def _L1_xattn_ref(x, latents, attention_mask, q_w, q_b, kv_w, kv_b, out_w, out_b, postnorm_w, mlp_w1, mlp_b1, mlp_w2, mlp_b2):
        import jax, jax.numpy as jnp
        import numpy as np
        B, P, K, H, NH = (4, 512, 64, 512, 16)
        DH = H // NH
        EPS = 1e-06

        def rmsnorm(x, w):
            var = jnp.mean(jnp.square(x), axis=-1, keepdims=True)
            return x * jax.lax.rsqrt(var + EPS) * w
        b, p, _ = x.shape
        k_len = latents.shape[1]
        residual = latents
        h = jnp.concatenate([x, latents], axis=1)
        q = (latents @ q_w + q_b).reshape(b, k_len, NH, DH)
        kv = (h @ kv_w + kv_b).reshape(b, p + k_len, NH, DH, 2)
        kmat, v = (kv[..., 0], kv[..., 1])
        attn = jnp.einsum('bkhd,bnhd->bhkn', q, kmat) / DH
        full_mask = jnp.concatenate([attention_mask.astype(bool), jnp.ones((b, k_len), bool)], axis=-1)
        attn = jnp.where(full_mask[:, None, None, :], attn, -jnp.inf)
        attn = jax.nn.softmax(attn.astype(jnp.float32), axis=-1).astype(q.dtype)
        attn_out = jnp.einsum('bhkn,bnhd->bkhd', attn, v).reshape(b, k_len, H)
        attn_out = attn_out @ out_w + out_b + residual
        out = rmsnorm(attn_out, postnorm_w)
        out = jax.nn.gelu(out @ mlp_w1 + mlp_b1) @ mlp_w2 + mlp_b2
        return out + residual
    x = _L0_xattn_ref(x, ctx_2048, L0_xattn_Wq, L0_xattn_bq, L0_xattn_Wk, L0_xattn_bk, L0_xattn_Wv, L0_xattn_bv)
    x = _L1_xattn_ref(ctx_2048, x, mask_BxS2_ik0, L1_xattn_q_w, L1_xattn_q_b, L1_xattn_kv_w, L1_xattn_kv_b, L1_xattn_out_w, L1_xattn_out_b, L1_xattn_postnorm_w, L1_xattn_mlp_w1, L1_xattn_mlp_b1, L1_xattn_mlp_w2, L1_xattn_mlp_b2)
    return x

_drawn_inputs = setup_inputs


def setup_inputs(seed=0):
    import zlib

    import numpy as np

    out = dict(_drawn_inputs(seed))
    spreads = {'L1_xattn_q_b': (0.0, 0.8),
     'L1_xattn_kv_b': (0.0, 0.8),
     'L1_xattn_out_b': (0.0, 1.912),
     'L1_xattn_postnorm_w': (1.0, 0.2),
     'L1_xattn_mlp_b1': (0.0, 0.1),
     'L1_xattn_mlp_b2': (0.0, 0.1)}
    factors = {'L0_xattn_bk': 64.0, 'L1_xattn_q_w': 8.0, 'L1_xattn_kv_w': 8.0, 'L1_xattn_out_w': 5.733}
    for name, (base, spread) in spreads.items():
        noise = np.random.default_rng([zlib.crc32(name.encode()), seed]).standard_normal(out[name].shape)
        drawn = base * np.exp(spread * noise) if base else spread * noise
        out[name] = jnp.asarray(drawn.astype(out[name].dtype))
    for name, factor in factors.items():
        out[name] = (out[name] * factor).astype(out[name].dtype)
    return out
```

```python
from contextlib import ExitStack

import numpy as np
import concourse.bass as bass
from concourse import mybir

F32 = mybir.dt.float32
F32R = mybir.dt.float32r
F16 = mybir.dt.float16
BF16 = mybir.dt.bfloat16
I32 = mybir.dt.int32
ALU = mybir.AluOpType
ACT = mybir.ActivationFunctionType
AX = mybir.AxisListType

P = 128
B, C, N = 16, 256, 512
H, D = 16, 32
HQ = 4
QUARTERS = H // HQ
HC = N // P
TB = 2 * C // P
QB = C // P
SW = 3 * D + 1
VW = 3 * D
UNITS = H * QB
MASKED = -float(2 ** 126)
F = 4 * N
FB = F // P
TILES = B * C // N
TT = N // P
EPS = 1e-6

L0_USES = ["q", "k", "v0", "v1", "S0", "S1", "T0", "T1", "A0", "S2", "S3", "T2", "T3", "A1"]
L0_N = len(L0_USES)
L0_V = [u for u in L0_USES if u[0] != "S"]
L0_HI = [u for u in L0_USES if u[0] in "qkvT"]

P_USES = [("cT0", "V"), ("cT1", "V"), ("lT0", "V"), ("lT1", "V"), ("Q0", "V"), ("Q1", "V")]
P_USES += [(f"Qs{i}", "AV"[i % 2]) for i in range(H // 2)]
for _q in range(QUARTERS):
    P_USES += [(f"KV{_q}0", "V"), (f"KV{_q}1", "V")] + [(f"Ks{_q}{i}", "AV"[i % 2]) for i in range(HQ)]
P_USES += [("aT0", "V"), ("aT1", "V"), ("o0", "V"), ("o1", "V")]
P_N = len(P_USES)
P_IDX = {name: i for i, (name, _) in enumerate(P_USES)}
P_DRAINS = {e: [name for name, d in P_USES if d == e] for e in "VA"}
P_HI = ["cT0", "cT1", "lT0", "lT1", "aT0", "aT1"]
TMPS = ["Q0", "Q1"] + [f"KV{q}{i}" for q in range(QUARTERS) for i in range(2)]


def upto(names, name):
    return names.index(name) + 1


def load_weights(nc, stage, wts, raws, consts):
    with ExitStack() as ctx:
        stages = [ctx.enter_context(nc.sbuf_tensor(f"{stage}_stage{i}", list(hi.shape), F32))
                  for i, (hi, lo, src, scale) in enumerate(wts)]
        raw_loaded = [ctx.enter_context(nc.semaphore(f"{stage}_raw_loaded{i}")) for i in range(len(wts))]
        consts_loaded = ctx.enter_context(nc.semaphore(f"{stage}_consts_loaded"))
        hi_ready = ctx.enter_context(nc.semaphore(f"{stage}_w_hi_ready"))
        lo_ready = ctx.enter_context(nc.semaphore(f"{stage}_w_lo_ready"))
        with nc.Block() as block:
            @block.sync
            def _(sp):
                for dst, src in consts:
                    sp.dma_start(dst, src).then_inc(consts_loaded, 16)
                for st, (hi, lo, src, scale), s in zip(stages, wts, raw_loaded):
                    sp.dma_start(st[:], src).then_inc(s, 16)

            @block.scalar
            def _(act):
                act.wait_ge(consts_loaded, 16 * len(consts))
                for i, (st, (hi, lo, src, scale)) in enumerate(zip(stages, wts)):
                    act.wait_ge(raw_loaded[i], 16)
                    act.activation(hi[:], st[:], ACT.Identity, scale=scale).then_inc(hi_ready, 1)

            @block.vector
            def _(dve):
                dve.wait_ge(consts_loaded, 16 * len(consts))
                for i, (st, (hi, lo, src, scale)) in enumerate(zip(stages, wts)):
                    dve.wait_ge(hi_ready, i + 1)
                    dve.scalar_tensor_tensor(out=lo[:], in0=st[:], scalar=scale, in1=hi[:].bitcast(F32),
                                             op0=ALU.mult, op1=ALU.subtract).then_inc(lo_ready, 1)
                raws(dve, consts_loaded, 16 * len(consts))


def build(nc, x, ctx_in, mask, wq3, bq3, wk3, bk3, wvT, bv, q_w, q_b, kv_w, kv_b, out_w, out_b,
          post_w, w1, b1, w2, b2, ident, out):
    lat_dram = nc.dram_tensor("lat_scratch", [B * C, N], F32, kind="Internal").ap()
    mid_dram = nc.dram_tensor("mid_scratch", [B * C, N], F32, kind="Internal").ap()
    with ExitStack() as both:
        ssq = both.enter_context(nc.sbuf_tensor("ssq", [P, B * QB], F32))
        rms = both.enter_context(nc.sbuf_tensor("rms", [P, B * QB], F32))
        idn = both.enter_context(nc.sbuf_tensor("idn", [P, P], F32))
        stage_a(nc, x, ctx_in, mask, wq3, bq3, wk3, bk3, wvT, bv, q_w, q_b, kv_w, kv_b, out_w, out_b,
                ident, lat_dram, mid_dram, ssq, idn)
        stage_b(nc, post_w, w1, b1, w2, b2, lat_dram, mid_dram, ssq, rms, idn, out)


def stage_a(nc, x, ctx_in, mask, wq3, bq3, wk3, bk3, wvT, bv, q_w, q_b, kv_w, kv_b, out_w, out_b,
            ident, lat_dram, mid_dram, ssq, idn):
    with ExitStack() as ctx:
        def sb(name, shape, dt=F32):
            return ctx.enter_context(nc.sbuf_tensor(name, shape, dt))

        def sem(name):
            return ctx.enter_context(nc.semaphore(name))

        def pair(name, shape):
            return sb(name + "_hi", shape, F32R), sb(name + "_lo", shape, F32R)

        wq_t, wk_t, wv_t = pair("wq_t", [P, QB, 3 * D]), pair("wk_t", [P, QB, 3 * D]), pair("wv_t", [P, QB, C])
        qw, kvw, ow = pair("qw", [P, HC, N]), pair("kvw", [P, HC, 2 * N]), pair("ow", [P, HC, N])
        idr = sb("idr", [P, P], F32R)
        bq = sb("bq", [3 * D, 1])
        bk = sb("bk", [3 * D, 1])
        bvc = sb("bvc", [P, QB])
        qb_row = sb("qb_row", [P, N])
        kvb_row = sb("kvb_row", [P, 2 * N])
        ob_row = sb("ob_row", [P, N])

        def chunks(w):
            return w.rearrange("(c p) m -> p c m", p=P)

        ones_col = sb("ones_col", [P, 1])
        ready = sem("setup_done")

        def raws(dve, sem_, value):
            dve.memset(ones_col[:], 1.0).then_inc(ready, 1)
            dve.wait_ge(sem_, value)
            dve.tensor_copy(idr[:], idn[:]).then_inc(ready, 1)
            dve.tensor_scalar(qb_row[:], qb_row[:], 1.0 / D, None, ALU.mult).then_inc(ready, 1)
            dve.wait_ge(ready, 3)

        load_weights(
            nc, "a",
            [(*wq_t, chunks(wq3), 1.0), (*wk_t, chunks(wk3), 1.0), (*wv_t, chunks(wvT), 1.0),
             (*qw, chunks(q_w), 1.0 / D), (*kvw, chunks(kv_w), 1.0), (*ow, chunks(out_w), 1.0)],
            raws,
            [(idn[:], ident), (bq[:], bq3), (bk[:], bk3), (bvc[:], bv),
             (qb_row[:], q_b.partition_broadcast(P)), (kvb_row[:], kv_b.partition_broadcast(P)),
             (ob_row[:], out_b.partition_broadcast(P))])

        x_raw = sb("x_raw", [P, QB, N])
        ctx_raw = sb("ctx_raw", [P, QB, N])
        mask_raw = sb("mask_raw", [P, QB], I32)
        mask_bias = sb("mask_bias", [P, TB])
        turn = pair("turn", [P, QB * N])
        x_s = [t[:, :].rearrange("p (c n) -> p c n", c=QB) for t in turn]
        vT_s = [t[:, :].rearrange("p (m c) -> p m c", m=HC) for t in turn]
        aT_s = [t[:, :].rearrange("p (c q) -> p c q", c=HC) for t in turn]
        ctx_s = pair("ctx_s", [P, QB, N])
        p0 = sb("p0", [P, 2, N])
        q_region = sb("q_region", [P, QB * H * SW], F32R)
        q_tok = q_region[:, :].rearrange("p (q h s) -> p q h s", q=QB, h=H)
        q0_stack = q_region[0:3 * D, 0:N]
        k0_stack = q_region[0:3 * D, N:2 * N]
        pT0 = [q_region[:, 2 * N + i * HC * 256:2 * N + (i + 1) * HC * 256].rearrange("p (m n) -> p m n", m=HC)
               for i in range(2)] if 2 * N + 2 * HC * 256 <= QB * H * SW else None
        lat = sb("lat", [P, QB, N])
        lat_b = sb("lat_b", [P, QB, N])
        hT = pair("hT", [P, HC, TB * P])
        q_stack = sb("q_stack", [SW, H, C], F32R)
        k_tok = sb("k_tok", [P, TB, HQ, SW], F32R)
        k_stack = sb("k_stack", [SW, 2, HQ, TB * P], F32R)
        tmp = sb("tmp", [P, 2, N])
        vs = sb("vs", [P, 2, TB, HQ, VW], BF16)
        prob = sb("prob", [P, 2, TB * P])
        pT_hi = sb("pT_hi", [P, 2, TB, P], F16)
        pT_lo = sb("pT_lo", [P, 2, TB, P], F16)
        attn = sb("attn", [P, QB, N])
        o_sum = sb("o_sum", [P, 4, D])
        nmax0, sum0, rec0 = sb("nmax0", [P, HC]), sb("sum0", [P, HC]), sb("rec0", [P, HC])
        nmax, sums, rec = sb("nmax", [P, UNITS]), sb("sums", [P, UNITS]), sb("rec", [P, 4])

        ps = [ctx.enter_context(nc.psum_tensor(f"bank{i}", [P, N], F32)) for i in range(8)]
        bank_s, bank_t, bank_p, bank_o, bank_0 = ps[0:2], ps[2:4], ps[4:6], ps[6], ps[7]

        loaded = sem("inputs_loaded")
        split_hi, split_lo = sem("split_hi"), sem("split_lo")
        l0_filled, l0_hi, l0_drained = sem("l0_filled"), sem("l0_hi"), sem("l0_drained")
        l0_max, l0_exp, l0_rec, l0_norm = sem("l0_max"), sem("l0_exp"), sem("l0_rec"), sem("l0_norm")
        lat_stored, lat_b_ready, mask_ready = sem("lat_stored"), sem("lat_b_ready"), sem("mask_ready")
        p_filled, p_hi = sem("p_filled"), sem("p_hi")
        p_drained = {"V": sem("p_drained_v"), "A": sem("p_drained_a")}
        tmp_hi, tmp_used, g_step = sem("tmp_hi"), sem("tmp_used"), sem("g_step")
        s_filled, s_max, s_exp = sem("s_filled"), sem("s_max"), sem("s_exp")
        t_filled, t_hi, t_lo = sem("t_filled"), sem("t_hi"), sem("t_lo")
        av_filled, o_summed, o_ready = sem("av_filled"), sem("o_summed"), sem("o_ready")
        mid_stored, squared, g_rec, zero_ready = sem("mid_stored"), sem("squared"), sem("g_rec"), sem("zero_ready")

        SPLIT3 = ((0, 0), (1, 0), (0, 1))

        def l0_at(b, name):
            return b * L0_N + upto(L0_USES, name)

        def l0_v(b, name):
            return b * len(L0_V) + upto(L0_V, name)

        def p_at(b, name):
            return b * P_N + P_IDX[name] + 1

        def p_dr(b, name):
            d = dict(P_USES)[name]
            return p_drained[d], b * len(P_DRAINS[d]) + upto(P_DRAINS[d], name)

        def p_bank(name):
            return bank_p[P_IDX[name] % 2]

        block = ctx.enter_context(nc.Block())

        @block.sync
        def _(sp):
            with sp.Fori(0, B) as b:
                sp.wait_ge(p_filled, b * P_N)
                sp.dma_start(ctx_raw[:], ctx_in[b].rearrange("(t p) n -> p t n", p=P)).then_inc(loaded, 16)
                sp.dma_start(x_raw[:], x[b].rearrange("(t p) n -> p t n", p=P)).then_inc(loaded, 16)
                sp.dma_start(mask_raw[:], mask[b]).then_inc(loaded, 16)
                sp.wait_ge(l0_drained, l0_v(b, "A1"))
                sp.dma_start(lat_dram.rearrange("(b t p) n -> b p t n", p=P, t=QB)[b], lat[:]).then_inc(lat_stored, 16)
                sp.wait_ge(*p_dr(b, "o1"))
                sp.dma_start(mid_dram.rearrange("(b t p) n -> b p t n", p=P, t=QB)[b], lat_b[:]).then_inc(mid_stored, 16)
            sp.wait_ge(lat_stored, 16 * B)
            sp.wait_ge(mid_stored, 16 * B)

        @block.tensor
        def _(pe):
            def l0_free(b, name):
                i = L0_USES.index(name)
                if i == 0:
                    pe.wait_ge(l0_drained, b * len(L0_V))
                elif L0_USES[i - 1][0] == "S":
                    pe.wait_ge(l0_exp, b * HC + int(L0_USES[i - 1][1]) + 1)
                else:
                    pe.wait_ge(l0_drained, l0_v(b, L0_USES[i - 1]))

            def l0_project(b, name, w, src, part):
                l0_free(b, name)
                pe.wait_ge(split_lo, b * 2 + part)
                for i, (wp, mp) in enumerate(SPLIT3):
                    for c in range(QB):
                        mm = pe.matmul(bank_0[0:3 * D, :], w[wp][:, c, :], src[mp][:, c, :],
                                       start=(i == 0 and c == 0), stop=(i == 2 and c == QB - 1))
                mm.then_inc(l0_filled, 1)

            def l0_values(b, j):
                l0_free(b, f"v{j}")
                for t in range(2):
                    m = 2 * j + t
                    for i, (wp, mp) in enumerate(SPLIT3):
                        for c in range(QB):
                            mm = pe.matmul(bank_0[:, t * C:(t + 1) * C], ctx_s[mp][:, c, m * P:(m + 1) * P],
                                           wv_t[wp][:, c, :], start=(i == 0 and c == 0),
                                           stop=(i == 2 and c == QB - 1))
                mm.then_inc(l0_filled, 1)

            def l0_scores(b, nb):
                l0_free(b, f"S{nb}")
                pe.matmul(bank_0[:, :], q0_stack[:, nb * P:(nb + 1) * P], k0_stack[:, :],
                          start=True, stop=True).then_inc(l0_filled, 1)

            def l0_turn(b, nb):
                l0_free(b, f"T{nb}")
                pe.wait_ge(l0_norm, b * HC + nb + 1)
                for m in range(HC):
                    mm = pe.transpose(bank_0[:, m * P:(m + 1) * P], p0[:, nb % 2, m * P:(m + 1) * P], idn[:])
                mm.then_inc(l0_filled, 1)

            def l0_out(b, half):
                l0_free(b, f"A{half}")
                for cb in range(QB):
                    for i, (wp, mp) in enumerate(SPLIT3):
                        for m in range(HC):
                            mm = pe.matmul(bank_0[:, cb * C:(cb + 1) * C], vT_s[wp][:, m, cb * P:(cb + 1) * P],
                                           pT0[mp][:, m, :], start=(i == 0 and m == 0),
                                           stop=(i == 2 and m == HC - 1))
                mm.then_inc(l0_filled, 1)

            def p_free(b, name):
                i = P_IDX[name]
                if i < 2:
                    pe.wait_ge(p_drained["V"], b * len(P_DRAINS["V"]))
                else:
                    pe.wait_ge(*p_dr(b, P_USES[i - 2][0]))

            def turn(b, name, src, blk):
                p_free(b, name)
                for hc in range(HC):
                    mm = pe.transpose(p_bank(name)[:, hc * P:(hc + 1) * P], src[:, blk, hc * P:(hc + 1) * P], idn[:])
                mm.then_inc(p_filled, 1)

            def project(b, name, parts, w, cols):
                p_free(b, name)
                bank = p_bank(name)
                for o, (src, t) in enumerate(parts):
                    width = cols.stop - cols.start
                    for i, (wp, mp) in enumerate(SPLIT3):
                        for hc in range(HC):
                            mm = pe.matmul(bank[:, o * width:(o + 1) * width], src[mp][:, hc, t * P:(t + 1) * P],
                                           w[wp][:, hc, cols], start=(i == 0 and hc == 0),
                                           stop=(i == 2 and hc == HC - 1))
                mm.then_inc(p_filled, 1)

            def stack_q(b, i):
                p_free(b, f"Qs{i}")
                if i == 0:
                    pe.wait_ge(tmp_used, b * len(TMPS) + 2)
                for j in range(4):
                    mm = pe.transpose(p_bank(f"Qs{i}")[0:SW, j * P:(j + 1) * P].bitcast(F32R),
                                      q_tok[:, j % 2, 2 * i + j // 2, :], idr[:])
                mm.then_inc(p_filled, 1)

            def stack_k(b, q, i):
                p_free(b, f"Ks{q}{i}")
                if i == 0:
                    pe.wait_ge(tmp_used, b * len(TMPS) + upto(TMPS, f"KV{q}1"))
                for t in range(TB):
                    mm = pe.transpose(p_bank(f"Ks{q}{i}")[0:SW, t * P:(t + 1) * P].bitcast(F32R),
                                      k_tok[:, t, i, :], idr[:])
                mm.then_inc(p_filled, 1)

            def keys_values(b, q, half):
                project(b, f"KV{q}{half}", [(hT, 2 * half), (hT, 2 * half + 1)], kvw, slice(q * 256, q * 256 + 256))

            def scores(b, u):
                h = u // QB
                if u >= 2:
                    pe.wait_ge(s_exp, b * UNITS + u - 1)
                else:
                    pe.wait_ge(s_exp, b * UNITS)
                if u % 2 == 0:
                    pe.wait_ge(*p_dr(b, f"Ks{h // HQ}{h % HQ}"))
                qb = u % QB
                pe.matmul(bank_s[u % 2][:, :], q_stack[:, h, qb * P:(qb + 1) * P],
                          k_stack[:, (h // HQ) % 2, h % HQ, :], start=True, stop=True).then_inc(s_filled, 1)

            def probs_turn(b, u):
                pe.wait_ge(s_exp, b * UNITS + u + 1)
                pe.wait_ge(t_lo, b * UNITS + max(u - 1, 0))
                for t in range(TB):
                    mm = pe.transpose(bank_t[u % 2][:, t * P:(t + 1) * P], prob[:, u % 2, t * P:(t + 1) * P], idn[:])
                mm.then_inc(t_filled, 1)

            def weigh(b, u):
                h = u // QB
                pe.wait_ge(t_lo, b * UNITS + u + 1)
                if u % 4 == 0:
                    pe.wait_ge(o_summed, b * (UNITS // 4) + u // 4)
                if u % (2 * HQ) == 0:
                    pe.wait_ge(tmp_used, b * len(TMPS) + upto(TMPS, f"KV{h // HQ}1"))
                o = (u % 4) * VW
                v = vs[:, (h // HQ) % 2, :, h % HQ, :]
                pe.matmul(bank_o[:, o:o + VW], pT_hi[:, u % 2, 0, :], v[:, 0, :], start=True, stop=False)
                for t in range(TB):
                    pe.matmul(bank_o[:, o:o + 2 * D], pT_lo[:, u % 2, t, :], v[:, t, 0:2 * D], start=False, stop=False)
                for t in range(1, TB):
                    mm = pe.matmul(bank_o[:, o:o + VW], pT_hi[:, u % 2, t, :], v[:, t, :],
                                   start=False, stop=(t == TB - 1))
                mm.then_inc(av_filled, 1)

            with pe.Fori(0, B) as b:
                l0_project(b, "q", wq_t, x_s, 1)
                l0_project(b, "k", wk_t, ctx_s, 2)
                l0_values(b, 0)
                l0_values(b, 1)
                for half in range(2):
                    l0_scores(b, 2 * half)
                    l0_scores(b, 2 * half + 1)
                    l0_turn(b, 2 * half)
                    l0_turn(b, 2 * half + 1)
                    l0_out(b, half)
                turn(b, "cT0", ctx_raw, 0)
                turn(b, "cT1", ctx_raw, 1)
                pe.wait_ge(l0_drained, l0_v(b, "A1"))
                turn(b, "lT0", lat, 0)
                turn(b, "lT1", lat, 1)
                pe.wait_ge(*p_dr(b, "lT1"))
                project(b, "Q0", [(hT, 2)], qw, slice(0, N))
                project(b, "Q1", [(hT, 3)], qw, slice(0, N))
                keys = 0
                for i in range(H // 2):
                    stack_q(b, i)
                keys_values(b, 0, 0)
                keys_values(b, 0, 1)
                for i in range(HQ):
                    stack_k(b, 0, i)
                for s in range(UNITS + 2):
                    if s < UNITS:
                        scores(b, s)
                    if 1 <= s <= UNITS:
                        probs_turn(b, s - 1)
                    if s >= 2:
                        weigh(b, s - 2)
                    q, at = s // 8 + 1, s % 8
                    if q < QUARTERS and at in (3, 4):
                        keys_values(b, q, at - 3)
                    if q < QUARTERS and at in (5, 6):
                        stack_k(b, q, 2 * (at - 5))
                        stack_k(b, q, 2 * (at - 5) + 1)
                pe.wait_ge(o_ready, b * (UNITS // 4) + UNITS // 4)
                turn(b, "aT0", attn, 0)
                turn(b, "aT1", attn, 1)
                pe.wait_ge(*p_dr(b, "aT0"))
                project(b, "o0", [(aT_s, 0)], ow, slice(0, N))
                pe.wait_ge(*p_dr(b, "aT1"))
                project(b, "o1", [(aT_s, 1)], ow, slice(0, N))

        @block.scalar
        def _(act):
            def l0_round(b, name, out_, in_, bias=None):
                act.wait_ge(l0_filled, l0_at(b, name))
                if bias is None:
                    ins = act.activation(out_, in_, ACT.Copy)
                else:
                    ins = act.activation(out_, in_, ACT.Identity, bias=bias)
                ins.then_inc(l0_hi, 1)

            def l0_soft(b, nb):
                act.wait_ge(l0_max, b * HC + nb + 1)
                act.activation(p0[:, nb % 2, :], bank_0[:, :], ACT.Exp, bias=nmax0[:, nb:nb + 1],
                               accum_out=sum0[:, nb:nb + 1]).then_inc(l0_exp, 1)

            def p_round(b, name, out_):
                act.wait_ge(p_filled, p_at(b, name))
                act.activation(out_, p_bank(name)[:, :].rearrange("p (c t) -> p c t", c=HC),
                               ACT.Copy).then_inc(p_hi, 1)

            def q_round(b, qb):
                act.wait_ge(*p_dr(b, f"Q{qb}"))
                src = tmp[:, qb, :].rearrange("p (h d) -> p h d", d=D)
                for part in range(2):
                    ins = act.activation(q_tok[:, qb, :, part * D:(part + 1) * D], src, ACT.Copy)
                ins.then_inc(tmp_hi, 1)

            def k_round(b, q, half):
                k = upto(TMPS, f"KV{q}{half}")
                act.wait_ge(*p_dr(b, f"KV{q}{half}"))
                src = tmp[:, (k - 1) % 2, 0:256].rearrange("p (a d) -> p a d", d=D)
                dst = k_tok[:, 2 * half:2 * half + 2, :, :].rearrange("p t h s -> p (t h) s")
                act.activation(dst[:, :, 0:D], src, ACT.Copy)
                act.activation(dst[:, :, 2 * D:3 * D], src, ACT.Copy)
                act.wait_ge(av_filled, b * UNITS + max(q - 1, 0) * 2 * HQ)
                act.activation(vs[:, q % 2, 2 * half:2 * half + 2, :, 0:D].rearrange("p t h s -> p (t h) s"),
                               tmp[:, (k - 1) % 2, 256:512].rearrange("p (a d) -> p a d", d=D),
                               ACT.Copy).then_inc(tmp_hi, 1)

            def drain_q(b, i):
                act.wait_ge(p_filled, p_at(b, f"Qs{i}"))
                act.activation(q_stack[:, 2 * i:2 * i + 2, :],
                               p_bank(f"Qs{i}")[0:SW, :].rearrange("p (h q) -> p h q", h=2),
                               ACT.Copy).then_inc(p_drained["A"], 1)

            def drain_k(b, q, i):
                act.wait_ge(p_filled, p_at(b, f"Ks{q}{i}"))
                act.activation(k_stack[:, q % 2, i, :], p_bank(f"Ks{q}{i}")[0:SW, :],
                               ACT.Copy).then_inc(p_drained["A"], 1)

            def soft(b, u):
                act.wait_ge(s_max, b * UNITS + u + 1)
                act.wait_ge(t_filled, b * UNITS + max(u - 1, 0))
                act.activation(prob[:, u % 2, :], bank_s[u % 2][:, :], ACT.Exp, bias=nmax[:, u:u + 1],
                               accum_out=sums[:, u:u + 1]).then_inc(s_exp, 1)

            def prob_round(b, u):
                act.wait_ge(t_filled, b * UNITS + u + 1)
                act.wait_ge(av_filled, b * UNITS + max(u - 1, 0))
                act.activation(pT_hi[:, u % 2, :, :], bank_t[u % 2][:, :].rearrange("p (t q) -> p t q", t=TB),
                               ACT.Copy).then_inc(t_hi, 1)

            with act.Fori(0, B) as b:
                act.wait_ge(loaded, b * 48 + 48)
                act.wait_ge(p_filled, b * P_N)
                act.activation(x_s[0], x_raw[:], ACT.Copy).then_inc(split_hi, 1)
                act.activation(ctx_s[0][:], ctx_raw[:], ACT.Copy).then_inc(split_hi, 1)
                l0_round(b, "q", q0_stack, bank_0[0:3 * D, :], bq[:, 0:1])
                l0_round(b, "k", k0_stack, bank_0[0:3 * D, :], bk[:, 0:1])
                for j in range(2):
                    l0_round(b, f"v{j}", vT_s[0][:, 2 * j:2 * j + 2, :], bank_0[:, :].rearrange("p (m c) -> p m c", m=2))
                for half in range(2):
                    l0_soft(b, 2 * half)
                    l0_soft(b, 2 * half + 1)
                    for j in range(2):
                        l0_round(b, f"T{2 * half + j}", pT0[0][:, :, j * P:(j + 1) * P],
                                 bank_0[:, :].rearrange("p (m n) -> p m n", m=HC))
                for t, name in enumerate(("cT0", "cT1", "lT0", "lT1")):
                    p_round(b, name, hT[0][:, :, t * P:(t + 1) * P])
                q_round(b, 0)
                q_round(b, 1)
                for i in range(0, H // 2, 2):
                    drain_q(b, i)
                k_round(b, 0, 0)
                k_round(b, 0, 1)
                for i in range(0, HQ, 2):
                    drain_k(b, 0, i)
                for s in range(UNITS + 1):
                    if s < UNITS:
                        soft(b, s)
                    if s >= 1:
                        prob_round(b, s - 1)
                    q, at = s // 8 + 1, s % 8
                    if q < QUARTERS and at in (3, 4):
                        k_round(b, q, at - 3)
                    if q < QUARTERS and at in (5, 6):
                        drain_k(b, q, 2 * (at - 5))
                for qb in range(QB):
                    p_round(b, f"aT{qb}", aT_s[0][:, :, qb * P:(qb + 1) * P])
                for qb in range(QB):
                    act.wait_ge(*p_dr(b, f"o{qb}"))
                    act.activation(attn[:, qb, :], lat_b[:, qb, :], ACT.Square,
                                   accum_out=ssq[:, bass.ds(b * QB + qb, 1)]).then_inc(squared, 1)

        @block.vector
        def _(dve):
            def split_rest(b, k, out_, raw, hi):
                dve.wait_ge(split_hi, b * 2 + k)
                dve.tensor_tensor(out_, raw, hi.bitcast(F32), ALU.subtract).then_inc(split_lo, 1)

            def l0_rest(b, name, out_, in_, hi):
                dve.wait_ge(l0_hi, b * len(L0_HI) + upto(L0_HI, name))
                dve.tensor_tensor(out_, in_, hi.bitcast(F32), ALU.subtract).then_inc(l0_drained, 1)

            def l0_stack_rest(b, name, stack, rows, bias):
                dve.wait_ge(l0_hi, b * len(L0_HI) + upto(L0_HI, name))
                dve.scalar_tensor_tensor(out=stack[rows, :], in0=bank_0[rows, :], scalar=bias[rows, 0:1],
                                         in1=stack[rows, :].bitcast(F32), op0=ALU.add,
                                         op1=ALU.subtract).then_inc(l0_drained, 1)

            def l0_peak(b, nb):
                dve.wait_ge(l0_filled, l0_at(b, f"S{nb}"))
                dve.tensor_reduce(nmax0[:, nb:nb + 1], bank_0[:, :], AX.X, ALU.max, negate=True).then_inc(l0_max, 1)

            def l0_normalise(b, nb):
                dve.wait_ge(l0_exp, b * HC + nb + 1)
                dve.reciprocal(rec0[:, nb:nb + 1], sum0[:, nb:nb + 1]).then_inc(l0_rec, 1)
                dve.wait_ge(l0_rec, b * HC + nb + 1)
                dve.tensor_scalar(p0[:, nb % 2, :], p0[:, nb % 2, :], rec0[:, nb:nb + 1], None,
                                  ALU.mult).then_inc(l0_norm, 1)

            def l0_latents(b, half):
                dve.wait_ge(l0_filled, l0_at(b, f"A{half}"))
                if half == 0:
                    dve.wait_ge(lat_stored, b * 16)
                    dve.wait_ge(lat_b_ready, b * 1)
                for cb in range(QB):
                    ins = dve.scalar_tensor_tensor(
                        out=lat[:, cb, half * C:(half + 1) * C], in0=bank_0[:, cb * C:(cb + 1) * C],
                        scalar=bvc[:, cb:cb + 1], in1=x_raw[:, cb, half * C:(half + 1) * C],
                        op0=ALU.add, op1=ALU.add)
                ins.then_inc(l0_drained, 1)

            def p_rest(b, name, out_, hi):
                dve.wait_ge(p_hi, b * len(P_HI) + upto(P_HI, name))
                dve.tensor_tensor(out_, p_bank(name)[:, :].rearrange("p (c t) -> p c t", c=HC), hi.bitcast(F32),
                                  ALU.subtract).then_inc(p_drained["V"], 1)

            def add_bias(b, name):
                k = TMPS.index(name)
                dve.wait_ge(p_filled, p_at(b, name))
                dve.wait_ge(tmp_used, b * len(TMPS) + max(k - 1, 0))
                if name[0] == "Q":
                    out_, in_, row = tmp[:, k % 2, :], p_bank(name)[:, :], qb_row[:, :]
                else:
                    q = int(name[2])
                    out_ = tmp[:, k % 2, :].rearrange("p (v t e) -> p v t e", v=2, t=2)
                    in_ = p_bank(name)[:, :].rearrange("p (t v e) -> p v t e", v=2, t=2)
                    row = kvb_row[:, q * 256:(q + 1) * 256].rearrange("p (v o e) -> p v o e", v=2, o=1)
                    row = row.to_broadcast([P, 2, 2, P])
                dve.tensor_tensor(out_, in_, row, ALU.add).then_inc(p_drained["V"], 1)

            def drain_q(b, i):
                dve.wait_ge(p_filled, p_at(b, f"Qs{i}"))
                dve.tensor_copy(q_stack[:, 2 * i:2 * i + 2, :],
                                p_bank(f"Qs{i}")[0:SW, :].rearrange("p (h q) -> p h q", h=2)
                                ).then_inc(p_drained["V"], 1)

            def drain_k(b, q, i):
                dve.wait_ge(p_filled, p_at(b, f"Ks{q}{i}"))
                dve.tensor_copy(k_stack[:, q % 2, i, :], p_bank(f"Ks{q}{i}")[0:SW, :]).then_inc(p_drained["V"], 1)

            def peak(b, u):
                dve.wait_ge(s_filled, b * UNITS + u + 1)
                dve.tensor_reduce(nmax[:, u:u + 1], bank_s[u % 2][:, :], AX.X, ALU.max, negate=True).then_inc(s_max, 1)

            def prob_rest(b, u):
                dve.wait_ge(t_hi, b * UNITS + u + 1)
                dve.tensor_tensor(pT_lo[:, u % 2, :, :], bank_t[u % 2][:, :].rearrange("p (t q) -> p t q", t=TB),
                                  pT_hi[:, u % 2, :, :], ALU.subtract).then_inc(t_lo, 1)

            def heads_out(b, g):
                n = UNITS // 4
                dve.wait_ge(av_filled, b * UNITS + 4 * g + 4)
                dve.reciprocal(rec[:, :], sums[:, 4 * g:4 * g + 4]).then_inc(g_rec, 1)
                dve.tensor_reduce(o_sum[:, :, :],
                                  bank_o[:, 0:4 * VW].rearrange("p (u v d) -> p u d v", u=4, v=3),
                                  AX.X, ALU.add).then_inc(o_summed, 1)
                dve.wait_ge(g_rec, b * n + g + 1)
                dve.wait_ge(o_summed, b * n + g + 1)
                for hh in range(2):
                    ins = dve.tensor_tensor(
                        attn[:, :, (2 * g + hh) * D:(2 * g + hh + 1) * D], o_sum[:, 2 * hh:2 * hh + 2, :],
                        rec[:, 2 * hh:2 * hh + 2].rearrange("p (q o) -> p q o", o=1).to_broadcast([P, 2, D]),
                        ALU.mult)
                ins.then_inc(o_ready, 1)
                dve.wait_ge(o_ready, b * n + g + 1)

            with dve.Fori(0, B) as b:
                dve.wait_ge(loaded, b * 48 + 48)
                dve.wait_ge(tmp_used, b * len(TMPS))
                dve.tensor_scalar(mask_bias[:, 0:QB], mask_raw[:, :], 0.0, MASKED, ALU.is_equal,
                                  ALU.mult).then_inc(mask_ready, 1)
                split_rest(b, 1, x_s[1], x_raw[:], x_s[0])
                split_rest(b, 2, ctx_s[1][:], ctx_raw[:], ctx_s[0][:])
                l0_stack_rest(b, "q", q0_stack, slice(2 * D, 3 * D), bq)
                l0_stack_rest(b, "k", k0_stack, slice(D, 2 * D), bk)
                for j in range(2):
                    l0_rest(b, f"v{j}", vT_s[1][:, 2 * j:2 * j + 2, :],
                            bank_0[:, :].rearrange("p (m c) -> p m c", m=2), vT_s[0][:, 2 * j:2 * j + 2, :])
                for half in range(2):
                    for nb in (2 * half, 2 * half + 1):
                        l0_peak(b, nb)
                        l0_normalise(b, nb)
                    for j in range(2):
                        l0_rest(b, f"T{2 * half + j}", pT0[1][:, :, j * P:(j + 1) * P],
                                bank_0[:, :].rearrange("p (m n) -> p m n", m=HC), pT0[0][:, :, j * P:(j + 1) * P])
                    l0_latents(b, half)
                for t, name in enumerate(("cT0", "cT1", "lT0", "lT1")):
                    p_rest(b, name, hT[1][:, :, t * P:(t + 1) * P], hT[0][:, :, t * P:(t + 1) * P])
                add_bias(b, "Q0")
                add_bias(b, "Q1")
                for i in range(1, H // 2, 2):
                    drain_q(b, i)
                add_bias(b, "KV00")
                add_bias(b, "KV01")
                for i in range(1, HQ, 2):
                    drain_k(b, 0, i)
                for s in range(UNITS + 2):
                    if s < UNITS:
                        peak(b, s)
                    if 1 <= s <= UNITS:
                        prob_rest(b, s - 1)
                    if s >= 2 and (s - 2) % 4 == 3:
                        heads_out(b, (s - 2) // 4)
                    q, at = s // 8 + 1, s % 8
                    if q < QUARTERS and at in (3, 4):
                        add_bias(b, f"KV{q}{at - 3}")
                    if q < QUARTERS and at in (5, 6):
                        drain_k(b, q, 2 * (at - 5) + 1)
                for qb in range(QB):
                    p_rest(b, f"aT{qb}", aT_s[1][:, :, qb * P:(qb + 1) * P], aT_s[0][:, :, qb * P:(qb + 1) * P])
                for qb in range(QB):
                    dve.wait_ge(p_filled, p_at(b, f"o{qb}"))
                    dve.wait_ge(lat_b_ready, b + 1)
                    dve.tensor_tensor(lat_b[:, qb, :], p_bank(f"o{qb}")[:, :], lat_b[:, qb, :],
                                      ALU.add).then_inc(p_drained["V"], 1)

        @block.gpsimd
        def _(pool):
            pool.memset(mask_bias[:, QB:TB], 0.0).then_inc(zero_ready, 1)
            pool.wait_ge(zero_ready, 1)
            with pool.Fori(0, B) as b:
                pool.wait_ge(mask_ready, b + 1)
                pool.wait_ge(l0_drained, l0_v(b, "A1"))
                pool.wait_ge(mid_stored, b * 16)
                pool.wait_ge(squared, b * 2)
                for qb in range(QB):
                    ins = pool.tensor_tensor(lat_b[:, qb, :], lat[:, qb, :], ob_row[:, :], ALU.add)
                ins.then_inc(lat_b_ready, 1)
                for k, name in enumerate(TMPS):
                    q = int(name[2]) if name[0] == "K" else 0
                    pool.wait_ge(tmp_hi, b * len(TMPS) + k + 1)
                    if name[0] == "Q":
                        dst = q_tok[:, k, :, :]
                        src = tmp[:, k % 2, :].rearrange("p (h d) -> p h d", d=D)
                        pool.tensor_tensor(dst[:, :, 2 * D:3 * D], src, dst[:, :, 0:D].bitcast(F32), ALU.subtract)
                        pool.tensor_copy(dst[:, :, 3 * D:SW], ones_col[:, :].rearrange("p (a o) -> p a o", o=1)
                                         .to_broadcast([P, H, 1])).then_inc(tmp_used, 1)
                        continue
                    half = int(name[3])
                    src = tmp[:, k % 2, 0:256].rearrange("p (a d) -> p a d", d=D)
                    dst = k_tok[:, 2 * half:2 * half + 2, :, :].rearrange("p t h s -> p (t h) s")
                    pool.tensor_tensor(dst[:, :, D:2 * D], src, dst[:, :, 0:D].bitcast(F32), ALU.subtract)
                    for t in range(2 * half, 2 * half + 2):
                        pool.tensor_copy(k_tok[:, t, :, 3 * D:SW],
                                         mask_bias[:, t:t + 1].rearrange("p (a o) -> p a o", o=1)
                                         .to_broadcast([P, HQ, 1]))
                    val = tmp[:, k % 2, 256:512].rearrange("p (a d) -> p a d", d=D)
                    v = vs[:, q % 2, 2 * half:2 * half + 2, :, :].rearrange("p t h s -> p (t h) s")
                    n = b * (2 * QUARTERS * 2) + (k - 2) * 2
                    pool.tensor_tensor(v[:, :, D:2 * D], val, v[:, :, 0:D], ALU.subtract).then_inc(g_step, 1)
                    pool.wait_ge(g_step, n + 1)
                    pool.tensor_tensor(val, val, v[:, :, 0:D], ALU.subtract).then_inc(g_step, 1)
                    pool.wait_ge(g_step, n + 2)
                    pool.tensor_tensor(v[:, :, 2 * D:3 * D], val, v[:, :, D:2 * D], ALU.subtract).then_inc(tmp_used, 1)


def stage_b(nc, post_w, w1, b1, w2, b2, lat_dram, mid_dram, ssq, rms, idn, out):
    with ExitStack() as ctx:
        def sb(name, shape, dt=F32):
            return ctx.enter_context(nc.sbuf_tensor(name, shape, dt))

        def sem(name):
            return ctx.enter_context(nc.semaphore(name))

        w1_s = sb("w1_hi", [P, HC, F], F32R), sb("w1_lo", [P, HC, F], F32R)
        w2_s = sb("w2_hi", [P, FB, N], F32R), sb("w2_lo", [P, FB, N], F32R)
        pw = sb("pw", [P, HC])
        b1c = sb("b1c", [P, FB])
        b2_row = sb("b2_row", [P, N])
        w1_in = w1.rearrange("(c p) m -> p c m", p=P)
        w2_in = w2.rearrange("(f p) m -> p f m", p=P)
        quarter = FB // 4
        load_weights(
            nc, "b",
            [(w1_s[0][:, c, :], w1_s[1][:, c, :], w1_in[:, c, :], pw[:, c:c + 1]) for c in range(HC)] +
            [(*(w[:, f * quarter:(f + 1) * quarter, :] for w in w2_s), w2_in[:, f * quarter:(f + 1) * quarter, :], 1.0)
             for f in range(4)],
            lambda dve, sem_, value: None,
            [(pw[:], post_w), (b1c[:], b1), (b2_row[:], b2.partition_broadcast(P))])

        mid = sb("mid", [P, TT, N])
        res = sb("res", [P, TT, N])
        hT = sb("hTn_hi", [P, HC, N], F32R), sb("hTn_lo", [P, HC, N], F32R)
        g = sb("g", [P, 2, N])
        g_s = sb("g_hi", [P, 2, N], F32R), sb("g_lo", [P, 2, N], F32R)
        ps = [ctx.enter_context(nc.psum_tensor(f"b_bank{i}", [P, N], F32)) for i in range(8)]
        bank_d, bank_o = ps[0:4], ps[4:8]

        mean, root, inverse = sem("mean"), sem("root"), sem("inverse")
        mid_loaded, res_loaded, res_ready, stored = sem("mid_loaded"), sem("res_loaded"), sem("res_ready"), sem("stored")
        normed, turned, turn_hi, turn_lo = sem("normed"), sem("turned"), sem("turn_hi"), sem("turn_lo")
        up_filled, gelu_done, g_rounded, g_ready = sem("up_filled"), sem("gelu_done"), sem("g_rounded"), sem("g_ready")
        down_done, out_filled, out_ready = sem("down_done"), sem("out_filled"), sem("out_ready")
        SPLIT3 = ((0, 0), (1, 0), (0, 1))

        def tokens(a, t):
            return a.rearrange("(t j p) n -> t p j n", p=P, j=TT)[t]

        block = ctx.enter_context(nc.Block())

        @block.sync
        def _(sp):
            def tile(t, more):
                sp.wait_ge(stored, t * 16)
                sp.dma_start(res[:], tokens(lat_dram, t)).then_inc(res_loaded, 16)
                if more:
                    sp.wait_ge(turned, t * TT + TT)
                    sp.dma_start(mid[:], tokens(mid_dram, t + 1)).then_inc(mid_loaded, 16)
                sp.wait_ge(out_ready, t * TT + TT)
                sp.dma_start(tokens(out, t), res[:]).then_inc(stored, 16)

            sp.dma_start(mid[:], tokens(mid_dram, 0)).then_inc(mid_loaded, 16)
            with sp.Fori(0, TILES - 1) as t:
                tile(t, True)
            tile(TILES - 1, False)
            sp.wait_ge(stored, 16 * TILES)

        @block.tensor
        def _(pe):
            def turn(t, first=False):
                pe.wait_ge(normed, t * TT + TT)
                for j in range(TT):
                    if not first:
                        pe.wait_ge(gelu_done, t * FB - TT + j + 1)
                    for hc in range(HC):
                        mm = pe.transpose(bank_d[j][:, hc * P:(hc + 1) * P], mid[:, j, hc * P:(hc + 1) * P], idn[:])
                    mm.then_inc(turned, 1)

            def up(t, f):
                if f == 0:
                    pe.wait_ge(turn_lo, t * TT + TT)
                if f >= TT:
                    pe.wait_ge(gelu_done, t * FB + f - TT + 1)
                for i, (wp, mp) in enumerate(SPLIT3):
                    for hc in range(HC):
                        mm = pe.matmul(bank_d[f % 4][:, :], w1_s[wp][:, hc, f * P:(f + 1) * P], hT[mp][:, hc, :],
                                       start=(i == 0 and hc == 0), stop=(i == 2 and hc == HC - 1))
                mm.then_inc(up_filled, 1)

            def down(t, f):
                pe.wait_ge(g_ready, t * FB + f + 1)
                if f == 0:
                    pe.wait_ge(out_ready, t * TT)
                for j in range(TT):
                    for i, (gp, wp) in enumerate(SPLIT3):
                        mm = pe.matmul(bank_o[j][:, :], g_s[gp][:, f % 2, j * P:(j + 1) * P], w2_s[wp][:, f, :],
                                       start=(f == 0 and i == 0), stop=(f == FB - 1 and i == 2))
                    if f == FB - 1:
                        mm.then_inc(out_filled, 1)
                    elif j == TT - 1:
                        mm.then_inc(down_done, 1)

            def tile(t, more):
                for f in range(FB):
                    up(t, f)
                    if f == FB - 1 and more:
                        turn(t + 1)
                    if f:
                        down(t, f - 1)
                down(t, FB - 1)

            turn(0, first=True)
            with pe.Fori(0, TILES - 1) as t:
                tile(t, True)
            tile(TILES - 1, False)

        @block.scalar
        def _(act):
            act.wait_ge(mean, 1)
            act.activation(rms[:], ssq[:], ACT.Sqrt).then_inc(root, 1)

            def turn_round(t):
                for j in range(TT):
                    act.wait_ge(turned, t * TT + j + 1)
                    act.activation(hT[0][:, :, j * P:(j + 1) * P], bank_d[j][:, :].rearrange("p (c t) -> p c t", c=HC),
                                   ACT.Copy).then_inc(turn_hi, 1)

            def tile(t, more):
                for f in range(FB):
                    act.wait_ge(up_filled, t * FB + f + 1)
                    act.wait_ge(g_ready, t * FB + max(f - 1, 0))
                    act.activation(g[:, f % 2, :], bank_d[f % 4][:, :], ACT.Gelu_apprx_tanh,
                                   bias=b1c[:, f:f + 1]).then_inc(gelu_done, 1)
                if more:
                    turn_round(t + 1)

            turn_round(0)
            with act.Fori(0, TILES - 1) as t:
                tile(t, True)
            tile(TILES - 1, False)

        @block.vector
        def _(dve):
            dve.tensor_scalar(ssq[:], ssq[:], 1.0 / N, EPS, ALU.mult, ALU.add).then_inc(mean, 1)
            dve.wait_ge(root, 1)
            dve.reciprocal(rms[:], rms[:]).then_inc(inverse, 1)
            dve.wait_ge(inverse, 1)

            def norm(t):
                dve.wait_ge(mid_loaded, t * 16 + 16)
                for j in range(TT):
                    dve.tensor_scalar(mid[:, j, :], mid[:, j, :], rms[:, bass.ds(t * TT + j, 1)], None,
                                      ALU.mult).then_inc(normed, 1)

            def turn_rest(t):
                for j in range(TT):
                    dve.wait_ge(turn_hi, t * TT + j + 1)
                    dve.tensor_tensor(hT[1][:, :, j * P:(j + 1) * P], bank_d[j][:, :].rearrange("p (c t) -> p c t", c=HC),
                                      hT[0][:, :, j * P:(j + 1) * P].bitcast(F32), ALU.subtract).then_inc(turn_lo, 1)

            def split(t, f):
                dve.wait_ge(gelu_done, t * FB + f + 1)
                if f >= 2:
                    dve.wait_ge(down_done, t * (FB - 1) + f - 1)
                else:
                    dve.wait_ge(out_filled, t * TT)
                dve.tensor_copy(g_s[0][:, f % 2, :], g[:, f % 2, :]).then_inc(g_rounded, 1)
                dve.wait_ge(g_rounded, t * FB + f + 1)
                dve.tensor_tensor(g_s[1][:, f % 2, :], g[:, f % 2, :], g_s[0][:, f % 2, :].bitcast(F32),
                                  ALU.subtract).then_inc(g_ready, 1)

            def tile(t, more):
                for f in range(FB):
                    split(t, f)
                    if f == FB // 2 and more:
                        norm(t + 1)
                if more:
                    turn_rest(t + 1)
                dve.wait_ge(res_ready, t + 1)
                for j in range(TT):
                    dve.wait_ge(out_filled, t * TT + j + 1)
                    dve.tensor_tensor(res[:, j, :], bank_o[j][:, :], res[:, j, :], ALU.add).then_inc(out_ready, 1)

            norm(0)
            turn_rest(0)
            with dve.Fori(0, TILES - 1) as t:
                tile(t, True)
            tile(TILES - 1, False)

        @block.gpsimd
        def _(pool):
            with pool.Fori(0, TILES) as t:
                pool.wait_ge(res_loaded, t * 16 + 16)
                for j in range(TT):
                    ins = pool.tensor_tensor(res[:, j, :], res[:, j, :], b2_row[:, :], ALU.add)
                ins.then_inc(res_ready, 1)


def kernel(x, ctx_2048, mask_BxS2_ik0, L0_xattn_Wq, L0_xattn_bq, L0_xattn_Wk, L0_xattn_bk, L0_xattn_Wv,
           L0_xattn_bv, L1_xattn_q_w, L1_xattn_q_b, L1_xattn_kv_w, L1_xattn_kv_b, L1_xattn_out_w,
           L1_xattn_out_b, L1_xattn_postnorm_w, L1_xattn_mlp_w1, L1_xattn_mlp_b1, L1_xattn_mlp_w2,
           L1_xattn_mlp_b2):
    import concourse.bacc as bacc
    from concourse.bass_utils import run_bass_kernel_spmd

    def stacked(a):
        return np.tile(np.asarray(a).T, (1, 3))

    def by_quarter(a):
        a = np.asarray(a)
        a = a.reshape(*a.shape[:-1], QUARTERS, HQ, D, 2)
        return np.moveaxis(a, -1, -3).reshape(*a.shape[:-4], 2 * N)

    def columns(a, n):
        return np.asarray(a).reshape(n, P).T

    arrays = dict(
        x=x, ctx_in=ctx_2048, mask=np.asarray(mask_BxS2_ik0).reshape(B, QB, P).transpose(0, 2, 1),
        wq3=stacked(L0_xattn_Wq), bq3=np.tile(np.asarray(L0_xattn_bq), 3).reshape(3 * D, 1),
        wk3=stacked(L0_xattn_Wk), bk3=np.tile(np.asarray(L0_xattn_bk), 3).reshape(3 * D, 1),
        wvT=np.asarray(L0_xattn_Wv).T, bv=columns(L0_xattn_bv, QB),
        q_w=L1_xattn_q_w, q_b=L1_xattn_q_b, kv_w=by_quarter(L1_xattn_kv_w), kv_b=by_quarter(L1_xattn_kv_b),
        out_w=L1_xattn_out_w, out_b=L1_xattn_out_b, post_w=columns(L1_xattn_postnorm_w, HC),
        w1=L1_xattn_mlp_w1, b1=columns(L1_xattn_mlp_b1, FB), w2=L1_xattn_mlp_w2, b2=L1_xattn_mlp_b2,
        ident=np.eye(P, dtype=np.float32))
    arrays = {f"in_{k}": np.ascontiguousarray(v) for k, v in arrays.items()}
    nc = bacc.Bacc("TRN2", target_bir_lowering=False, num_devices=1)
    args = [nc.dram_tensor(k, v.shape, mybir.dt.from_np(v.dtype), kind="ExternalInput").ap() for k, v in arrays.items()]
    result = nc.dram_tensor("result", (B * C, N), F32, kind="ExternalOutput").ap()
    build(nc, *args, result)
    r = run_bass_kernel_spmd(nc, [arrays], core_ids=[0])
    return r.results[0]["result"].reshape(B, C, N)
```

```python
from contextlib import ExitStack

import numpy as np
import concourse.bass as bass
from concourse import mybir

F32 = mybir.dt.float32
F32R = mybir.dt.float32r
F16 = mybir.dt.float16
BF16 = mybir.dt.bfloat16
I32 = mybir.dt.int32
ALU = mybir.AluOpType
ACT = mybir.ActivationFunctionType
AX = mybir.AxisListType

P = 128
B, C, N = 16, 256, 512
H, D = 16, 32
HQ = 4
QUARTERS = H // HQ
HC = N // P
TB = 2 * C // P
QB = C // P
SW = 3 * D + 1
VW = 3 * D
UNITS = H * QB
MASKED = -float(2 ** 126)
F = 4 * N
FB = F // P
TILES = B * C // N
TT = N // P
EPS = 1e-6

FILL = {s: [] for s in range(UNITS)}
FILL[0] = ["split", "res", "Ks02", "Ks03"]
FILL[1] = ["Qs6", "Qs7", "<KV10"]
FILL[2] = ["KV10", "zq"]
FILL[3] = ["<KV11", "zk"]
FILL[4] = ["KV11", "aT0"]
FILL[5] = ["aT1", "V10"]
FILL[6] = ["Ks10", "Ks11", "o0", "V11"]
FILL[7] = ["Ks12", "Ks13", "<o1"]
FILL[8] = ["<KV20", "o1"]
FILL[9] = ["KV20", "zv0"]
FILL[10] = ["<KV21", "zv1"]
FILL[11] = ["KV21", "zS0"]
FILL[12] = ["n0", "V20", "zS1"]
FILL[13] = ["Ks20", "Ks21", "n1", "zT0", "V21"]
FILL[14] = ["Ks22", "Ks23", "zT1"]
FILL[15] = ["<KV30", "<zA0"]
FILL[16] = ["KV30", "zA0"]
FILL[17] = ["<KV31", "zS2"]
FILL[18] = ["n2", "KV31", "zS3"]
FILL[19] = ["n3", "zT2"]
FILL[20] = ["Ks30", "Ks31", "zT3"]
FILL[21] = ["Ks32", "Ks33", "<zA1", "V30"]
FILL[22] = ["mask", "zA1", "cT0", "cT1", "V31"]
FILL[23] = ["lT0", "lT1"]
FILL[24] = ["Q0"]
FILL[25] = ["Q1"]
FILL[26] = ["KV00"]
FILL[27] = ["Qs0", "<KV01"]
FILL[28] = ["KV01", "Qs1"]
FILL[29] = ["Qs2", "Qs3"]
FILL[30] = ["Ks00", "Qs4", "V00"]
FILL[31] = ["Ks01", "Qs5", "V01"]
ORDER = [name for s in range(UNITS) for name in FILL[s]]
OUT = {"aT0", "aT1", "o0", "o1", "<o0", "<o1"}
PREV = OUT | {"res"}
NEXT = {n for n in ORDER if n in ("mask", "split", "<zA0", "<zA1", "<Q0", "<Q1") or n[0] in "zncl" or
        n[:-1] in ("KV0", "V0", "<KV0") or n in ("Ks00", "Ks01", "Q0", "Q1") or (n[:2] == "Qs" and int(n[2]) < 6)}

Z_USES = [n for n in ORDER if n[0] in "zao"]
Z_V = [n for n in Z_USES if n[1] != "S"]
Z_HI = [n for n in Z_USES if n[0] == "a" or n[:2] in ("zq", "zk", "zv", "zT")]

P_USES = [(n, "A" if n[:2] in ("Qs", "Ks") and int(n[-1]) % 2 else "V")
          for part in (True, False) for n in ORDER if n[0] in "clQK" and (n in NEXT) == part]
P_N = len(P_USES)
P_IDX = {name: i for i, (name, _) in enumerate(P_USES)}
P_DRAINER = dict(P_USES)
P_DRAINS = {e: [name for name, d in P_USES if d == e] for e in "VA"}
P_HI = ["cT0", "cT1", "lT0", "lT1"]
TMPS = [n for n, _ in P_USES if n in ("Q0", "Q1") or n[:2] == "KV"]
LAST_STEP = 10


def upto(names, name):
    return names.index(name) + 1


def after(engine, semaphore, value):
    if not isinstance(value, int) or value > 0:
        engine.wait_ge(semaphore, value)


def load_weights(nc, stage, wts, raws, consts):
    with ExitStack() as ctx:
        stages = [ctx.enter_context(nc.sbuf_tensor(f"{stage}_stage{i}", list(hi.shape), F32))
                  for i, (hi, lo, src, scale) in enumerate(wts)]
        raw_loaded = [ctx.enter_context(nc.semaphore(f"{stage}_raw_loaded{i}")) for i in range(len(wts))]
        consts_loaded = ctx.enter_context(nc.semaphore(f"{stage}_consts_loaded"))
        hi_ready = ctx.enter_context(nc.semaphore(f"{stage}_w_hi_ready"))
        lo_ready = ctx.enter_context(nc.semaphore(f"{stage}_w_lo_ready"))
        with nc.Block() as block:
            @block.sync
            def _(sp):
                for dst, src in consts:
                    sp.dma_start(dst, src).then_inc(consts_loaded, 16)
                for st, (hi, lo, src, scale), s in zip(stages, wts, raw_loaded):
                    sp.dma_start(st[:], src).then_inc(s, 16)

            @block.scalar
            def _(act):
                act.wait_ge(consts_loaded, 16 * len(consts))
                for i, (st, (hi, lo, src, scale)) in enumerate(zip(stages, wts)):
                    act.wait_ge(raw_loaded[i], 16)
                    act.activation(hi[:], st[:], ACT.Identity, scale=scale).then_inc(hi_ready, 1)

            @block.vector
            def _(dve):
                dve.wait_ge(consts_loaded, 16 * len(consts))
                for i, (st, (hi, lo, src, scale)) in enumerate(zip(stages, wts)):
                    dve.wait_ge(hi_ready, i + 1)
                    dve.scalar_tensor_tensor(out=lo[:], in0=st[:], scalar=scale, in1=hi[:].bitcast(F32),
                                             op0=ALU.mult, op1=ALU.subtract).then_inc(lo_ready, 1)
                raws(dve, consts_loaded, 16 * len(consts))


def build(nc, x, ctx_in, mask, wq3, bq3, wk3, bk3, wvT, bv, q_w, q_b, kv_w, kv_b, out_w, out_b,
          post_w, w1, b1, w2, b2, ident, out):
    lat_dram = nc.dram_tensor("lat_scratch", [B * C, N], F32, kind="Internal").ap()
    mid_dram = nc.dram_tensor("mid_scratch", [B * C, N], F32, kind="Internal").ap()
    with ExitStack() as both:
        ssq = both.enter_context(nc.sbuf_tensor("ssq", [P, B * QB], F32))
        rms = both.enter_context(nc.sbuf_tensor("rms", [P, B * QB], F32))
        idn = both.enter_context(nc.sbuf_tensor("idn", [P, P], F32))
        stage_a(nc, x, ctx_in, mask, wq3, bq3, wk3, bk3, wvT, bv, q_w, q_b, kv_w, kv_b, out_w, out_b,
                ident, lat_dram, mid_dram, ssq, idn)
        stage_b(nc, post_w, w1, b1, w2, b2, lat_dram, mid_dram, ssq, rms, idn, out)


def stage_a(nc, x, ctx_in, mask, wq3, bq3, wk3, bk3, wvT, bv, q_w, q_b, kv_w, kv_b, out_w, out_b,
            ident, lat_dram, mid_dram, ssq, idn):
    with ExitStack() as ctx:
        def sb(name, shape, dt=F32):
            return ctx.enter_context(nc.sbuf_tensor(name, shape, dt))

        def sem(name):
            return ctx.enter_context(nc.semaphore(name))

        def pair(name, shape):
            return sb(name + "_hi", shape, F32R), sb(name + "_lo", shape, F32R)

        wq_t, wk_t, wv_t = pair("wq_t", [P, QB, 3 * D]), pair("wk_t", [P, QB, 3 * D]), pair("wv_t", [P, QB, C])
        qw, kvw, ow = pair("qw", [P, HC, N]), pair("kvw", [P, HC, 2 * N]), pair("ow", [P, HC, N])
        idr = sb("idr", [P, P], F32R)
        bq = sb("bq", [3 * D, 1])
        bk = sb("bk", [3 * D, 1])
        bvc = sb("bvc", [P, QB])
        qb_row = sb("qb_row", [P, N])
        kvb_row = sb("kvb_row", [P, 2 * N])
        ob_row = sb("ob_row", [P, N])

        def chunks(w):
            return w.rearrange("(c p) m -> p c m", p=P)

        ones_col = sb("ones_col", [P, 1])
        ready = sem("setup_done")

        def raws(dve, sem_, value):
            dve.memset(ones_col[:], 1.0).then_inc(ready, 1)
            dve.wait_ge(sem_, value)
            dve.tensor_copy(idr[:], idn[:]).then_inc(ready, 1)
            dve.tensor_scalar(qb_row[:], qb_row[:], 1.0 / D, None, ALU.mult).then_inc(ready, 1)
            dve.wait_ge(ready, 3)

        load_weights(
            nc, "a",
            [(*wq_t, chunks(wq3), 1.0), (*wk_t, chunks(wk3), 1.0), (*wv_t, chunks(wvT), 1.0),
             (*qw, chunks(q_w), 1.0 / D), (*kvw, chunks(kv_w), 1.0), (*ow, chunks(out_w), 1.0)],
            raws,
            [(idn[:], ident), (bq[:], bq3), (bk[:], bk3), (bvc[:], bv),
             (qb_row[:], q_b.partition_broadcast(P)), (kvb_row[:], kv_b.partition_broadcast(P)),
             (ob_row[:], out_b.partition_broadcast(P))])

        x_raw = sb("x_raw", [P, QB, N])
        ctx_raw = sb("ctx_raw", [P, QB, N])
        mask_raw = sb("mask_raw", [P, QB], I32)
        mask_bias = sb("mask_bias", [P, TB])
        turn = pair("turn", [P, QB * N])
        x_s = [t[:, :].rearrange("p (c n) -> p c n", c=QB) for t in turn]
        vT_s = [t[:, :].rearrange("p (m c) -> p m c", m=HC) for t in turn]
        aT_s = [t[:, :].rearrange("p (c q) -> p c q", c=HC) for t in turn]
        ctx_s = pair("ctx_s", [P, QB, N])
        p0 = sb("p0", [P, 2, N])
        q_region = sb("q_region", [P, QB * H * SW], F32R)
        q_tok = q_region[:, :].rearrange("p (q h s) -> p q h s", q=QB, h=H)
        q0_stack = q_region[0:3 * D, 0:N]
        k0_stack = q_region[0:3 * D, N:2 * N]
        pT0 = [q_region[:, 2 * N + i * HC * 256:2 * N + (i + 1) * HC * 256].rearrange("p (m n) -> p m n", m=HC)
               for i in range(2)] if 2 * N + 2 * HC * 256 <= QB * H * SW else None
        lat = sb("lat", [P, QB, N])
        lat_b = sb("lat_b", [P, QB, N])
        hT = pair("hT", [P, HC, TB * P])
        q_stack = sb("q_stack", [SW, H, C], F32R)
        k_tok = sb("k_tok", [P, TB, HQ, SW], F32R)
        k_stack = sb("k_stack", [SW, 2, HQ, TB * P], F32R)
        tmp = sb("tmp", [P, 2, N])
        vs = sb("vs", [P, 2, TB, HQ, VW], BF16)
        prob = sb("prob", [P, 2, TB * P])
        pT_hi = sb("pT_hi", [P, 2, TB, P], F16)
        pT_lo = sb("pT_lo", [P, 2, TB, P], F16)
        attn = sb("attn", [P, QB, N])
        o_sum = sb("o_sum", [P, 4, D])
        nmax0, sum0, rec0 = sb("nmax0", [P, HC]), sb("sum0", [P, HC]), sb("rec0", [P, HC])
        nmax, sums, rec = sb("nmax", [P, UNITS]), sb("sums", [P, UNITS]), sb("rec", [P, 4])

        ps = [ctx.enter_context(nc.psum_tensor(f"bank{i}", [P, N], F32)) for i in range(8)]
        bank_s, bank_t, bank_p, bank_o, bank_0 = ps[0:2], ps[2:4], ps[4:6], ps[6], ps[7]

        loaded = sem("inputs_loaded")
        split_hi, split_lo = sem("split_hi"), sem("split_lo")
        z_filled, z_hi, z_drained = sem("z_filled"), sem("z_hi"), sem("z_drained_v")
        l0_max, l0_exp, l0_rec, l0_norm = sem("l0_max"), sem("l0_exp"), sem("l0_rec"), sem("l0_norm")
        lat_stored, lat_b_ready, mask_ready = sem("lat_stored"), sem("lat_b_ready"), sem("mask_ready")
        p_filled, p_hi = sem("p_filled"), sem("p_hi")
        p_drained = {"V": sem("p_drained_v"), "A": sem("p_drained_a")}
        tmp_hi, vals_hi, stacked, tmp_used, g_step = (sem("tmp_hi"), sem("vals_hi"), sem("stacked"), sem("tmp_used"),
                                                      sem("g_step"))
        s_filled, s_max, s_exp = sem("s_filled"), sem("s_max"), sem("s_exp")
        t_filled, t_hi, t_lo = sem("t_filled"), sem("t_hi"), sem("t_lo")
        av_filled, o_summed, o_ready = sem("av_filled"), sem("o_summed"), sem("o_ready")
        res_loaded = sem("res_loaded_a")
        mid_stored, squared, g_rec, zero_ready = sem("mid_stored"), sem("squared"), sem("g_rec"), sem("zero_ready")

        SPLIT3 = ((0, 0), (1, 0), (0, 1))

        def z_at(it, prev, more, uses, name):
            def n(p, m):
                return sum(u in PREV for u in uses) * p + sum(u not in PREV for u in uses) * m
            if isinstance(it, int):
                base = sum(n(i > 0, i < B - 1) for i in range(-1, it))
            else:
                base = n(0, 1) * 2 + (it - 1) * n(1, 1)
            live = [u for u in uses if (prev if u in PREV else more)]
            return base + (upto(live, name) if name else 0)

        def p_at(b, name):
            return b * P_N + P_IDX[name] + 1

        def p_dr(b, name):
            d = P_DRAINER[name]
            return p_drained[d], b * len(P_DRAINS[d]) + upto(P_DRAINS[d], name)

        def p_bank(name):
            return bank_p[P_IDX[name] % 2]

        def run(engine, step, fill, late=(), rest=None):
            def fills(names, b, prev, cur, more):
                for name in names:
                    if name in PREV and prev:
                        fill(name, b - 1, b, prev, more)
                    elif name in NEXT and more:
                        fill(name, b + 1, b, prev, more)
                    elif name not in PREV and name not in NEXT and cur:
                        fill(name, b, b, prev, more)

            def iteration(b, prev, cur, more, steps=UNITS):
                for s in range(steps):
                    step(b, s, prev, cur, more)
                    if s > 0:
                        fills([n for n in FILL[s - 1] if n in late], b, prev, cur, more)
                    if rest:
                        rest(b, s, prev, cur, more)
                    fills([n for n in FILL[s] if n not in late], b, prev, cur, more)

            fills([n for n in ORDER if n in NEXT], -1, False, False, True)
            iteration(0, False, True, True)
            with engine.Fori(1, B - 1) as b:
                iteration(b, True, True, True)
            iteration(B - 1, True, True, False)
            iteration(B, True, False, False, LAST_STEP)

        block = ctx.enter_context(nc.Block())

        @block.sync
        def _(sp):
            def load(b):
                sp.dma_start(ctx_raw[:], ctx_in[b].rearrange("(t p) n -> p t n", p=P)).then_inc(loaded, 16)
                sp.dma_start(x_raw[:], x[b].rearrange("(t p) n -> p t n", p=P)).then_inc(loaded, 16)
                sp.dma_start(mask_raw[:], mask[b]).then_inc(loaded, 16)

            def store_latents(n, it, prev):
                sp.wait_ge(z_drained, z_at(it, prev, True, Z_V, "zA1"))
                sp.dma_start(lat_dram.rearrange("(b t p) n -> b p t n", p=P, t=QB)[n], lat[:]).then_inc(lat_stored, 16)

            def residual(n):
                sp.wait_ge(lat_stored, 16 * n + 16)
                after(sp, squared, 16 * n)
                after(sp, mid_stored, 16 * n)
                sp.dma_start(lat_b[:], lat_dram.rearrange("(b t p) n -> b p t n", p=P, t=QB)[n]).then_inc(res_loaded, 16)

            def store_mid(n, it, more):
                sp.wait_ge(z_drained, z_at(it, True, more, Z_V, "o1"))
                sp.dma_start(mid_dram.rearrange("(b t p) n -> b p t n", p=P, t=QB)[n], lat_b[:]).then_inc(mid_stored, 16)

            def load_next(n):
                sp.wait_ge(p_filled, p_at(n - 1, "lT0"))
                load(n)

            load(0)
            store_latents(0, -1, False)
            load_next(1)
            store_latents(1, 0, False)
            load_next(2)
            with sp.Fori(1, B - 2) as b:
                residual(b - 1)
                store_mid(b - 1, b, True)
                store_latents(b + 1, b, True)
                load_next(b + 2)
            residual(B - 3)
            store_mid(B - 3, B - 2, True)
            store_latents(B - 1, B - 2, True)
            residual(B - 2)
            store_mid(B - 2, B - 1, False)
            residual(B - 1)
            store_mid(B - 1, B, False)
            sp.wait_ge(lat_stored, 16 * B)
            sp.wait_ge(mid_stored, 16 * B)

        @block.tensor
        def _(pe):
            def halves(name):
                return (0,) if name[0] == "<" else (1,) if "<" + name in ORDER else (0, 1)

            def z_free(n, it, prev, more, name):
                last = ([u for u in Z_USES[:Z_USES.index(name.strip("<"))] if (prev if u in PREV else more)] or [""])[-1]
                if last[1:2] == "S":
                    pe.wait_ge(l0_exp, n * HC + int(last[2]) + 1)
                else:
                    after(pe, z_drained, z_at(it, prev, more, Z_V, last))

            def l0_project(w, src):
                for i, (wp, mp) in enumerate(SPLIT3):
                    for c in range(QB):
                        mm = pe.matmul(bank_0[0:3 * D, :], w[wp][:, c, :], src[mp][:, c, :],
                                       start=(i == 0 and c == 0), stop=(i == 2 and c == QB - 1))
                return mm

            def l0_values(j):
                for t in range(2):
                    m = 2 * j + t
                    for i, (wp, mp) in enumerate(SPLIT3):
                        for c in range(QB):
                            mm = pe.matmul(bank_0[:, t * C:(t + 1) * C], ctx_s[mp][:, c, m * P:(m + 1) * P],
                                           wv_t[wp][:, c, :], start=(i == 0 and c == 0),
                                           stop=(i == 2 and c == QB - 1))
                return mm

            def l0_scores(nb):
                return pe.matmul(bank_0[:, :], q0_stack[:, nb * P:(nb + 1) * P], k0_stack[:, :],
                                 start=True, stop=True)

            def l0_turn(nb):
                for m in range(HC):
                    mm = pe.transpose(bank_0[:, m * P:(m + 1) * P], p0[:, nb % 2, m * P:(m + 1) * P], idn[:])
                return mm

            def l0_out(blocks):
                for cb in blocks:
                    for i, (wp, mp) in enumerate(SPLIT3):
                        for m in range(HC):
                            mm = pe.matmul(bank_0[:, cb * C:(cb + 1) * C], vT_s[wp][:, m, cb * P:(cb + 1) * P],
                                           pT0[mp][:, m, :], start=(i == 0 and m == 0),
                                           stop=(i == 2 and m == HC - 1))
                return mm

            def l0(n, it, prev, more, name):
                blocks = halves(name)
                if 0 in blocks:
                    z_free(n, it, prev, more, name)
                name = name.strip("<")
                kind, j = name[1], int(name[2:] or 0)
                if kind in "qk":
                    pe.wait_ge(split_lo, n * 2 + 1 + (kind == "k"))
                    mm = l0_project(wq_t, x_s) if kind == "q" else l0_project(wk_t, ctx_s)
                elif kind == "v":
                    mm = l0_values(j)
                elif kind == "S":
                    mm = l0_scores(j)
                elif kind == "T":
                    pe.wait_ge(l0_norm, n * HC + j + 1)
                    mm = l0_turn(j)
                else:
                    mm = l0_out(blocks)
                if 1 in blocks:
                    mm.then_inc(z_filled, 1)

            def p_free(b, name):
                i = P_IDX[name]
                if i < 2:
                    last, d = P_USES[i - 2]
                    after(pe, p_drained[d], (b - 1) * len(P_DRAINS[d]) + upto(P_DRAINS[d], last))
                else:
                    pe.wait_ge(*p_dr(b, P_USES[i - 2][0]))

            def turn(bank, src, blk):
                for hc in range(HC):
                    mm = pe.transpose(bank[:, hc * P:(hc + 1) * P], src[:, blk, hc * P:(hc + 1) * P], idn[:])
                return mm

            def project(bank, o, src, t, w, first):
                for i, (wp, mp) in enumerate(SPLIT3):
                    for hc in range(HC):
                        mm = pe.matmul(bank[:, o * 256:(o + 1) * 256], src[mp][:, hc, t * P:(t + 1) * P],
                                       w[wp][:, hc, first:first + 256], start=(i == 0 and hc == 0),
                                       stop=(i == 2 and hc == HC - 1))
                return mm

            def l1_fill(b, it, prev, more, name):
                blocks, name = halves(name), name.strip("<")
                bank = p_bank(name)
                if 0 in blocks:
                    p_free(b, name)
                if name[1] == "T":
                    if name == "lT0":
                        pe.wait_ge(z_drained, z_at(it, prev, more, Z_V, "zA1"))
                    mm = turn(bank, ctx_raw if name[0] == "c" else lat, int(name[2]))
                elif name in ("Q0", "Q1"):
                    if name == "Q0" and 0 in blocks:
                        pe.wait_ge(*p_dr(b, "lT1"))
                    for o in blocks:
                        mm = project(bank, o, hT, 2 + int(name[1]), qw, o * 256)
                elif name[:2] == "Qs":
                    i = int(name[2])
                    if i == 0:
                        pe.wait_ge(stacked, b * len(TMPS) + 2)
                    for j in range(4):
                        mm = pe.transpose(bank[0:SW, j * P:(j + 1) * P].bitcast(F32R),
                                          q_tok[:, j % 2, 2 * i + j // 2, :], idr[:])
                elif name[:2] == "KV":
                    q, half = int(name[2]), int(name[3])
                    for o in blocks:
                        mm = project(bank, o, hT, 2 * half + o, kvw, q * 256)
                else:
                    q, i = int(name[2]), int(name[3])
                    if i == 0:
                        pe.wait_ge(stacked, b * len(TMPS) + upto(TMPS, f"KV{q}1"))
                    for t in range(TB):
                        mm = pe.transpose(bank[0:SW, t * P:(t + 1) * P].bitcast(F32R), k_tok[:, t, i, :], idr[:])
                if 1 in blocks:
                    mm.then_inc(p_filled, 1)

            def out(b, it, prev, more, name):
                blocks = halves(name)
                if 0 in blocks:
                    z_free(b, it, prev, more, name)
                qb = int(name[-1])
                if name == "aT0":
                    pe.wait_ge(o_ready, b * (UNITS // 4) + UNITS // 4)
                if name[0] == "a":
                    mm = turn(bank_0, attn, qb)
                else:
                    for o in blocks:
                        mm = project(bank_0, o, aT_s, qb, ow, o * 256)
                if 1 in blocks:
                    mm.then_inc(z_filled, 1)

            def scores(b, u):
                h, qb = u // QB, u % QB
                after(pe, s_exp, b * UNITS + u - 1)
                if u % 2 == 0:
                    pe.wait_ge(*p_dr(b, f"Ks{h // HQ}{h % HQ}"))
                pe.matmul(bank_s[u % 2][:, :], q_stack[:, h, qb * P:(qb + 1) * P],
                          k_stack[:, (h // HQ) % 2, h % HQ, :], start=True, stop=True).then_inc(s_filled, 1)

            def probs_turn(b, u):
                pe.wait_ge(s_exp, b * UNITS + u + 1)
                after(pe, t_lo, b * UNITS + u - 1)
                for t in range(TB):
                    mm = pe.transpose(bank_t[u % 2][:, t * P:(t + 1) * P], prob[:, u % 2, t * P:(t + 1) * P], idn[:])
                mm.then_inc(t_filled, 1)

            def weigh(b, u):
                h = u % UNITS // QB
                pe.wait_ge(t_lo, b * UNITS + u + 1)
                if u % 4 == 0:
                    after(pe, o_summed, b * (UNITS // 4) + u // 4)
                if u % (2 * HQ) == 0:
                    pe.wait_ge(tmp_used, b * len(TMPS) + upto(TMPS, f"KV{h // HQ}1"))
                o = (u % 4) * VW
                v = vs[:, (h // HQ) % 2, :, h % HQ, :]
                pe.matmul(bank_o[:, o:o + VW], pT_hi[:, u % 2, 0, :], v[:, 0, :], start=True, stop=False)
                for t in range(TB):
                    pe.matmul(bank_o[:, o:o + 2 * D], pT_lo[:, u % 2, t, :], v[:, t, 0:2 * D], start=False, stop=False)
                for t in range(1, TB):
                    mm = pe.matmul(bank_o[:, o:o + VW], pT_hi[:, u % 2, t, :], v[:, t, :],
                                   start=False, stop=(t == TB - 1))
                mm.then_inc(av_filled, 1)

            def step(b, s, prev, cur, more):
                if cur:
                    scores(b, s)
                if cur if s >= 2 else prev:
                    probs_turn(b, s - 2)
                if cur if s >= 4 else prev:
                    weigh(b, s - 4)

            def fill(name, b, it, prev, more):
                if name in OUT:
                    out(b, it, prev, more, name)
                elif name.strip("<") in Z_USES:
                    l0(b, it, prev, more, name)
                elif name.strip("<") in P_IDX:
                    l1_fill(b, it, prev, more, name)

            run(pe, step, fill)

        @block.scalar
        def _(act):
            def split(n):
                act.wait_ge(loaded, n * 48 + 48)
                act.activation(x_s[0], x_raw[:], ACT.Copy).then_inc(split_hi, 1)
                act.activation(ctx_s[0][:], ctx_raw[:], ACT.Copy).then_inc(split_hi, 1)

            def l0(n, it, prev, more, name):
                kind, j = name[1], int(name[2:] or 0)
                if kind == "S":
                    act.wait_ge(l0_max, n * HC + j + 1)
                    act.activation(p0[:, j % 2, :], bank_0[:, :], ACT.Exp, bias=nmax0[:, j:j + 1],
                                   accum_out=sum0[:, j:j + 1]).then_inc(l0_exp, 1)
                elif kind != "A":
                    act.wait_ge(z_filled, z_at(it, prev, more, Z_USES, name))
                    if kind == "q":
                        ins = act.activation(q0_stack, bank_0[0:3 * D, :], ACT.Identity, bias=bq[:, 0:1])
                    elif kind == "k":
                        ins = act.activation(k0_stack, bank_0[0:3 * D, :], ACT.Identity, bias=bk[:, 0:1])
                    elif kind == "v":
                        ins = act.activation(vT_s[0][:, 2 * j:2 * j + 2, :],
                                             bank_0[:, :].rearrange("p (m c) -> p m c", m=2), ACT.Copy)
                    else:
                        ins = act.activation(pT0[0][:, :, j % 2 * P:(j % 2 + 1) * P],
                                             bank_0[:, :].rearrange("p (m n) -> p m n", m=HC), ACT.Copy)
                    ins.then_inc(z_hi, 1)

            def l1_fill(b, name):
                if name in P_HI:
                    t = P_HI.index(name)
                    act.wait_ge(p_filled, p_at(b, name))
                    act.activation(hT[0][:, :, t * P:(t + 1) * P],
                                   p_bank(name)[:, :].rearrange("p (c t) -> p c t", c=HC), ACT.Copy).then_inc(p_hi, 1)
                elif name in ("Q0", "Q1"):
                    qb = int(name[1])
                    act.wait_ge(*p_dr(b, name))
                    src = tmp[:, qb, :].rearrange("p (h d) -> p h d", d=D)
                    for part in range(2):
                        ins = act.activation(q_tok[:, qb, :, part * D:(part + 1) * D], src, ACT.Copy)
                    ins.then_inc(tmp_hi, 1)
                elif name[:2] == "KV":
                    q, half = int(name[2]), int(name[3])
                    k = TMPS.index(name)
                    act.wait_ge(*p_dr(b, name))
                    src = tmp[:, k % 2, 0:256].rearrange("p (a d) -> p a d", d=D)
                    dst = k_tok[:, 2 * half:2 * half + 2, :, :].rearrange("p t h s -> p (t h) s")
                    act.activation(dst[:, :, 0:D], src, ACT.Copy)
                    act.activation(dst[:, :, 2 * D:3 * D], src, ACT.Copy).then_inc(tmp_hi, 1)
                elif P_DRAINER[name] == "A":
                    act.wait_ge(p_filled, p_at(b, name))
                    src = p_bank(name)[0:SW, :]
                    if name[0] == "Q":
                        i = int(name[2])
                        ins = act.activation(q_stack[:, 2 * i:2 * i + 2, :], src.rearrange("p (h q) -> p h q", h=2), ACT.Copy)
                    else:
                        ins = act.activation(k_stack[:, int(name[2]) % 2, int(name[3]), :], src, ACT.Copy)
                    ins.then_inc(p_drained["A"], 1)

            def values(b, name):
                q, half = int(name[1]), int(name[2])
                k = TMPS.index("K" + name)
                after(act, av_filled, b * UNITS + (q - 1) * 2 * HQ)
                act.activation(vs[:, q % 2, 2 * half:2 * half + 2, :, 0:D].rearrange("p t h s -> p (t h) s"),
                               tmp[:, k % 2, 256:512].rearrange("p (a d) -> p a d", d=D),
                               ACT.Copy).then_inc(vals_hi, 1)

            def out(b, it, more, name):
                qb = int(name[-1])
                if name[0] == "a":
                    act.wait_ge(z_filled, z_at(it, True, more, Z_USES, name))
                    act.activation(aT_s[0][:, :, qb * P:(qb + 1) * P], bank_0[:, :].rearrange("p (c t) -> p c t", c=HC),
                                   ACT.Copy).then_inc(z_hi, 1)
                else:
                    act.wait_ge(z_drained, z_at(it, True, more, Z_V, name))
                    act.activation(p0[:, qb, :], lat_b[:, qb, :], ACT.Square,
                                   accum_out=ssq[:, bass.ds(b * QB + qb, 1)]).then_inc(squared, 8)

            def soft(b, u):
                act.wait_ge(s_max, b * UNITS + u + 1)
                after(act, t_filled, b * UNITS + u - 1)
                act.activation(prob[:, u % 2, :], bank_s[u % 2][:, :], ACT.Exp, bias=nmax[:, u:u + 1],
                               accum_out=sums[:, u:u + 1]).then_inc(s_exp, 1)

            def prob_round(b, u):
                act.wait_ge(t_filled, b * UNITS + u + 1)
                after(act, av_filled, b * UNITS + u - 1)
                act.activation(pT_hi[:, u % 2, :, :], bank_t[u % 2][:, :].rearrange("p (t q) -> p t q", t=TB),
                               ACT.Copy).then_inc(t_hi, 1)

            def step(b, s, prev, cur, more):
                if cur if s >= 3 else prev:
                    prob_round(b, s - 3)
                if cur:
                    soft(b, s)

            def fill(name, b, it, prev, more):
                if name == "split":
                    split(b)
                elif name in OUT and name in Z_USES:
                    out(b, it, more, name)
                elif name in Z_USES:
                    l0(b, it, prev, more, name)
                elif name[0] == "V":
                    values(b, name)
                elif name in P_IDX:
                    l1_fill(b, name)

            run(act, step, fill, TMPS + ["o0", "o1"])

        @block.vector
        def _(dve):
            def mask_to_bias(n):
                dve.wait_ge(loaded, n * 48 + 48)
                after(dve, stacked, n * len(TMPS))
                dve.tensor_scalar(mask_bias[:, 0:QB], mask_raw[:, :], 0.0, MASKED, ALU.is_equal,
                                  ALU.mult).then_inc(mask_ready, 1)

            def stack_rest(stack, rows, bias):
                return dve.scalar_tensor_tensor(out=stack[rows, :], in0=bank_0[rows, :], scalar=bias[rows, 0:1],
                                                in1=stack[rows, :].bitcast(F32), op0=ALU.add, op1=ALU.subtract)

            def l0(n, it, prev, more, name):
                kind, j = name[1], int(name[2:] or 0)
                if kind == "S":
                    dve.wait_ge(z_filled, z_at(it, prev, more, Z_USES, name))
                    dve.tensor_reduce(nmax0[:, j:j + 1], bank_0[:, :], AX.X, ALU.max, negate=True).then_inc(l0_max, 1)
                    return
                if kind == "A":
                    dve.wait_ge(z_filled, z_at(it, prev, more, Z_USES, name))
                    if j == 0:
                        after(dve, lat_stored, n * 16)
                    for cb in range(QB):
                        ins = dve.scalar_tensor_tensor(
                            out=lat[:, cb, j * C:(j + 1) * C], in0=bank_0[:, cb * C:(cb + 1) * C],
                            scalar=bvc[:, cb:cb + 1], in1=x_raw[:, cb, j * C:(j + 1) * C], op0=ALU.add, op1=ALU.add)
                    ins.then_inc(z_drained, 1)
                    return
                dve.wait_ge(z_hi, z_at(it, prev, more, Z_HI, name))
                if kind == "q":
                    ins = stack_rest(q0_stack, slice(2 * D, 3 * D), bq)
                elif kind == "k":
                    ins = stack_rest(k0_stack, slice(D, 2 * D), bk)
                elif kind == "v":
                    ins = dve.tensor_tensor(vT_s[1][:, 2 * j:2 * j + 2, :], bank_0[:, :].rearrange("p (m c) -> p m c", m=2),
                                            vT_s[0][:, 2 * j:2 * j + 2, :].bitcast(F32), ALU.subtract)
                else:
                    part = slice(j % 2 * P, (j % 2 + 1) * P)
                    ins = dve.tensor_tensor(pT0[1][:, :, part], bank_0[:, :].rearrange("p (m n) -> p m n", m=HC),
                                            pT0[0][:, :, part].bitcast(F32), ALU.subtract)
                ins.then_inc(z_drained, 1)

            def reciprocal(n, nb):
                dve.wait_ge(l0_exp, n * HC + nb + 1)
                dve.reciprocal(rec0[:, nb:nb + 1], sum0[:, nb:nb + 1]).then_inc(l0_rec, 1)

            def l1_fill(b, name):
                if name in P_HI:
                    t = P_HI.index(name)
                    part = slice(t * P, (t + 1) * P)
                    dve.wait_ge(p_hi, b * len(P_HI) + t + 1)
                    dve.tensor_tensor(hT[1][:, :, part], p_bank(name)[:, :].rearrange("p (c t) -> p c t", c=HC),
                                      hT[0][:, :, part].bitcast(F32), ALU.subtract).then_inc(p_drained["V"], 1)
                elif name in TMPS:
                    k = TMPS.index(name)
                    dve.wait_ge(p_filled, p_at(b, name))
                    after(dve, tmp_used, b * len(TMPS) + k - 1)
                    if name[0] == "Q":
                        out_, in_, row = tmp[:, k % 2, :], p_bank(name)[:, :], qb_row[:, :]
                    else:
                        q = int(name[2])
                        out_ = tmp[:, k % 2, :].rearrange("p (v t e) -> p v t e", v=2, t=2)
                        in_ = p_bank(name)[:, :].rearrange("p (t v e) -> p v t e", v=2, t=2)
                        row = kvb_row[:, q * 256:(q + 1) * 256].rearrange("p (v o e) -> p v o e", v=2, o=1)
                        row = row.to_broadcast([P, 2, 2, P])
                    dve.tensor_tensor(out_, in_, row, ALU.add).then_inc(p_drained["V"], 1)
                elif P_DRAINER[name] == "V":
                    dve.wait_ge(p_filled, p_at(b, name))
                    src = p_bank(name)[0:SW, :]
                    if name[0] == "Q":
                        i = int(name[2])
                        ins = dve.tensor_copy(q_stack[:, 2 * i:2 * i + 2, :], src.rearrange("p (h q) -> p h q", h=2))
                    else:
                        ins = dve.tensor_copy(k_stack[:, int(name[2]) % 2, int(name[3]), :], src)
                    ins.then_inc(p_drained["V"], 1)

            def out(b, it, more, name):
                qb = int(name[-1])
                if name[0] == "a":
                    dve.wait_ge(z_hi, z_at(it, True, more, Z_HI, name))
                    part = slice(qb * P, (qb + 1) * P)
                    dve.tensor_tensor(aT_s[1][:, :, part], bank_0[:, :].rearrange("p (c t) -> p c t", c=HC),
                                      aT_s[0][:, :, part].bitcast(F32), ALU.subtract).then_inc(z_drained, 1)
                else:
                    dve.wait_ge(z_filled, z_at(it, True, more, Z_USES, name))
                    dve.wait_ge(lat_b_ready, b + 1)
                    dve.tensor_tensor(lat_b[:, qb, :], bank_0[:, :], lat_b[:, qb, :], ALU.add).then_inc(z_drained, 1)

            def peak(b, u):
                dve.wait_ge(s_filled, b * UNITS + u + 1)
                dve.tensor_reduce(nmax[:, u:u + 1], bank_s[u % 2][:, :], AX.X, ALU.max, negate=True).then_inc(s_max, 1)

            def prob_rest(b, u):
                dve.wait_ge(t_hi, b * UNITS + u + 1)
                dve.tensor_tensor(pT_lo[:, u % 2, :, :], bank_t[u % 2][:, :].rearrange("p (t q) -> p t q", t=TB),
                                  pT_hi[:, u % 2, :, :], ALU.subtract).then_inc(t_lo, 1)

            def heads_out(b, g, prev, more):
                n = UNITS // 4
                i = g % n
                dve.wait_ge(av_filled, b * UNITS + 4 * g + 4)
                dve.reciprocal(rec[:, :], sums[:, 4 * i:4 * i + 4]).then_inc(g_rec, 1)
                dve.tensor_reduce(o_sum[:, :, :],
                                  bank_o[:, 0:4 * VW].rearrange("p (u v d) -> p u d v", u=4, v=3),
                                  AX.X, ALU.add).then_inc(o_summed, 1)
                dve.wait_ge(g_rec, b * n + g + 1)
                dve.wait_ge(o_summed, b * n + g + 1)
                if g == 0 and prev:
                    dve.wait_ge(z_filled, z_at(b, True, more, Z_USES, "aT1"))
                for hh in range(2):
                    ins = dve.tensor_tensor(
                        attn[:, :, (2 * i + hh) * D:(2 * i + hh + 1) * D], o_sum[:, 2 * hh:2 * hh + 2, :],
                        rec[:, 2 * hh:2 * hh + 2].rearrange("p (q o) -> p q o", o=1).to_broadcast([P, 2, D]),
                        ALU.mult)
                ins.then_inc(o_ready, 1)

            def step(b, s, prev, cur, more):
                if cur:
                    peak(b, s)

            def rest(b, s, prev, cur, more):
                if cur if s >= 3 else prev:
                    prob_rest(b, s - 3)
                if s % 4 == 3 and (cur if s >= 7 else prev):
                    heads_out(b, s // 4 - 1, prev, more)

            def fill(name, b, it, prev, more):
                if name == "mask":
                    mask_to_bias(b)
                elif name[0] == "n":
                    reciprocal(b, int(name[1]))
                elif name in OUT and name in Z_USES:
                    out(b, it, more, name)
                elif name in Z_USES:
                    l0(b, it, prev, more, name)
                elif name in P_IDX:
                    l1_fill(b, name)

            run(dve, step, fill, Z_V + P_HI, rest)

        @block.gpsimd
        def _(pool):
            def stack_rest(b, name):
                k = TMPS.index(name)
                pool.wait_ge(tmp_hi, b * len(TMPS) + k + 1)
                if name[0] == "Q":
                    dst = q_tok[:, k, :, :]
                    src = tmp[:, k % 2, :].rearrange("p (h d) -> p h d", d=D)
                    pool.tensor_tensor(dst[:, :, 2 * D:3 * D], src, dst[:, :, 0:D].bitcast(F32),
                                       ALU.subtract).then_inc(tmp_used, 1)
                    pool.tensor_copy(dst[:, :, 3 * D:SW], ones_col[:, :].rearrange("p (a o) -> p a o", o=1)
                                     .to_broadcast([P, H, 1])).then_inc(stacked, 1)
                    return
                half = int(name[3])
                if name == "KV00":
                    pool.wait_ge(mask_ready, b + 1)
                src = tmp[:, k % 2, 0:256].rearrange("p (a d) -> p a d", d=D)
                dst = k_tok[:, 2 * half:2 * half + 2, :, :].rearrange("p t h s -> p (t h) s")
                pool.tensor_tensor(dst[:, :, D:2 * D], src, dst[:, :, 0:D].bitcast(F32), ALU.subtract)
                for t in range(2 * half, 2 * half + 2):
                    ins = pool.tensor_copy(k_tok[:, t, :, 3 * D:SW], mask_bias[:, t:t + 1].rearrange(
                        "p (a o) -> p a o", o=1).to_broadcast([P, HQ, 1]))
                ins.then_inc(stacked, 1)

            def values_rest(b, name):
                q, half, k = int(name[2]), int(name[3]), TMPS.index(name)
                val = tmp[:, k % 2, 256:512].rearrange("p (a d) -> p a d", d=D)
                v = vs[:, q % 2, 2 * half:2 * half + 2, :, :].rearrange("p t h s -> p (t h) s")
                n = b * (2 * QUARTERS * 2) + (k - 2) * 2
                pool.wait_ge(vals_hi, b * 2 * QUARTERS + k - 1)
                pool.tensor_tensor(v[:, :, D:2 * D], val, v[:, :, 0:D], ALU.subtract).then_inc(g_step, 1)
                pool.wait_ge(g_step, n + 1)
                pool.tensor_tensor(val, val, v[:, :, 0:D], ALU.subtract).then_inc(g_step, 1)
                pool.wait_ge(g_step, n + 2)
                pool.tensor_tensor(v[:, :, 2 * D:3 * D], val, v[:, :, D:2 * D], ALU.subtract).then_inc(tmp_used, 1)

            def split(b):
                pool.wait_ge(split_hi, b * 2 + 1)
                pool.tensor_tensor(x_s[1], x_raw[:], x_s[0].bitcast(F32), ALU.subtract).then_inc(split_lo, 1)
                pool.wait_ge(split_hi, b * 2 + 2)
                pool.tensor_tensor(ctx_s[1][:], ctx_raw[:], ctx_s[0][:].bitcast(F32), ALU.subtract).then_inc(split_lo, 1)

            def normalise(b, nb):
                pool.wait_ge(l0_rec, b * HC + nb + 1)
                pool.tensor_tensor(p0[:, nb % 2, :], p0[:, nb % 2, :], rec0[:, nb:nb + 1].to_broadcast([P, N]),
                                   ALU.mult).then_inc(l0_norm, 1)

            def residual(b):
                pool.wait_ge(res_loaded, b * 16 + 16)
                for qb in range(QB):
                    ins = pool.tensor_tensor(lat_b[:, qb, :], lat_b[:, qb, :], ob_row[:, :], ALU.add)
                ins.then_inc(lat_b_ready, 1)

            pool.memset(mask_bias[:, QB:TB], 0.0).then_inc(zero_ready, 1)
            pool.wait_ge(zero_ready, 1)
            def step(b, s, prev, cur, more):
                pass

            def fill(name, b, it, prev, more):
                if name == "res":
                    residual(b)
                elif name == "split":
                    split(b)
                elif name[0] == "n":
                    normalise(b, int(name[1]))
                elif name[0] == "V":
                    values_rest(b, "K" + name)
                elif name in TMPS:
                    stack_rest(b, name)

            run(pool, step, fill)


def stage_b(nc, post_w, w1, b1, w2, b2, lat_dram, mid_dram, ssq, rms, idn, out):
    with ExitStack() as ctx:
        def sb(name, shape, dt=F32):
            return ctx.enter_context(nc.sbuf_tensor(name, shape, dt))

        def sem(name):
            return ctx.enter_context(nc.semaphore(name))

        w1_s = sb("w1_hi", [P, HC, F], F32R), sb("w1_lo", [P, HC, F], F32R)
        w2_s = sb("w2_hi", [P, FB, N], F32R), sb("w2_lo", [P, FB, N], F32R)
        pw = sb("pw", [P, HC])
        b1c = sb("b1c", [P, FB])
        b2_row = sb("b2_row", [P, N])
        w1_in = w1.rearrange("(c p) m -> p c m", p=P)
        w2_in = w2.rearrange("(f p) m -> p f m", p=P)
        quarter = FB // 4
        load_weights(
            nc, "b",
            [(w1_s[0][:, c, :], w1_s[1][:, c, :], w1_in[:, c, :], pw[:, c:c + 1]) for c in range(HC)] +
            [(*(w[:, f * quarter:(f + 1) * quarter, :] for w in w2_s), w2_in[:, f * quarter:(f + 1) * quarter, :], 1.0)
             for f in range(4)],
            lambda dve, sem_, value: None,
            [(pw[:], post_w), (b1c[:], b1), (b2_row[:], b2.partition_broadcast(P))])

        mid = sb("mid", [P, TT, N])
        res = sb("res", [P, TT, N])
        hT = sb("hTn_hi", [P, HC, N], F32R), sb("hTn_lo", [P, HC, N], F32R)
        g = sb("g", [P, 2, N])
        g_s = sb("g_hi", [P, 2, N], F32R), sb("g_lo", [P, 2, N], F32R)
        ps = [ctx.enter_context(nc.psum_tensor(f"b_bank{i}", [P, N], F32)) for i in range(8)]
        bank_d, bank_o = ps[0:4], ps[4:8]

        mean, root, inverse = sem("mean"), sem("root"), sem("inverse")
        mid_loaded, res_loaded, res_ready, stored = sem("mid_loaded"), sem("res_loaded"), sem("res_ready"), sem("stored")
        normed, turned, turn_hi, turn_lo = sem("normed"), sem("turned"), sem("turn_hi"), sem("turn_lo")
        up_filled, gelu_done, g_rounded, g_ready = sem("up_filled"), sem("gelu_done"), sem("g_rounded"), sem("g_ready")
        down_done, out_filled, out_ready = sem("down_done"), sem("out_filled"), sem("out_ready")
        SPLIT3 = ((0, 0), (1, 0), (0, 1))

        def tokens(a, t):
            return a.rearrange("(t j p) n -> t p j n", p=P, j=TT)[t]

        block = ctx.enter_context(nc.Block())

        @block.sync
        def _(sp):
            def tile(t, more):
                sp.wait_ge(stored, t * 16)
                sp.dma_start(res[:], tokens(lat_dram, t)).then_inc(res_loaded, 16)
                if more:
                    sp.wait_ge(turned, t * TT + TT)
                    sp.dma_start(mid[:], tokens(mid_dram, t + 1)).then_inc(mid_loaded, 16)
                sp.wait_ge(out_ready, t * TT + TT)
                sp.dma_start(tokens(out, t), res[:]).then_inc(stored, 16)

            sp.dma_start(mid[:], tokens(mid_dram, 0)).then_inc(mid_loaded, 16)
            with sp.Fori(0, TILES - 1) as t:
                tile(t, True)
            tile(TILES - 1, False)
            sp.wait_ge(stored, 16 * TILES)

        @block.tensor
        def _(pe):
            def turn(t, first=False):
                pe.wait_ge(normed, t * TT + TT)
                for j in range(TT):
                    if not first:
                        pe.wait_ge(gelu_done, t * FB - TT + j + 1)
                    for hc in range(HC):
                        mm = pe.transpose(bank_d[j][:, hc * P:(hc + 1) * P], mid[:, j, hc * P:(hc + 1) * P], idn[:])
                    mm.then_inc(turned, 1)

            def up(t, f):
                if f == 0:
                    pe.wait_ge(turn_lo, t * TT + TT)
                if f >= TT:
                    pe.wait_ge(gelu_done, t * FB + f - TT + 1)
                for i, (wp, mp) in enumerate(SPLIT3):
                    for hc in range(HC):
                        mm = pe.matmul(bank_d[f % 4][:, :], w1_s[wp][:, hc, f * P:(f + 1) * P], hT[mp][:, hc, :],
                                       start=(i == 0 and hc == 0), stop=(i == 2 and hc == HC - 1))
                mm.then_inc(up_filled, 1)

            def down(t, f):
                pe.wait_ge(g_ready, t * FB + f + 1)
                if f == 0:
                    pe.wait_ge(out_ready, t * TT)
                for j in range(TT):
                    for i, (gp, wp) in enumerate(SPLIT3):
                        mm = pe.matmul(bank_o[j][:, :], g_s[gp][:, f % 2, j * P:(j + 1) * P], w2_s[wp][:, f, :],
                                       start=(f == 0 and i == 0), stop=(f == FB - 1 and i == 2))
                    if f == FB - 1:
                        mm.then_inc(out_filled, 1)
                    elif j == TT - 1:
                        mm.then_inc(down_done, 1)

            def tile(t, more):
                for f in range(FB):
                    up(t, f)
                    if f == FB - 1 and more:
                        turn(t + 1)
                    if f:
                        down(t, f - 1)
                down(t, FB - 1)

            turn(0, first=True)
            with pe.Fori(0, TILES - 1) as t:
                tile(t, True)
            tile(TILES - 1, False)

        @block.scalar
        def _(act):
            act.wait_ge(mean, 1)
            act.activation(rms[:], ssq[:], ACT.Sqrt).then_inc(root, 1)

            def turn_round(t):
                for j in range(TT):
                    act.wait_ge(turned, t * TT + j + 1)
                    act.activation(hT[0][:, :, j * P:(j + 1) * P], bank_d[j][:, :].rearrange("p (c t) -> p c t", c=HC),
                                   ACT.Copy).then_inc(turn_hi, 1)

            def tile(t, more):
                for f in range(FB):
                    act.wait_ge(up_filled, t * FB + f + 1)
                    act.wait_ge(g_ready, t * FB + max(f - 1, 0))
                    act.activation(g[:, f % 2, :], bank_d[f % 4][:, :], ACT.Gelu_apprx_tanh,
                                   bias=b1c[:, f:f + 1]).then_inc(gelu_done, 1)
                if more:
                    turn_round(t + 1)

            turn_round(0)
            with act.Fori(0, TILES - 1) as t:
                tile(t, True)
            tile(TILES - 1, False)

        @block.vector
        def _(dve):
            dve.tensor_scalar(ssq[:], ssq[:], 1.0 / N, EPS, ALU.mult, ALU.add).then_inc(mean, 1)
            dve.wait_ge(root, 1)
            dve.reciprocal(rms[:], rms[:]).then_inc(inverse, 1)
            dve.wait_ge(inverse, 1)

            def norm(t):
                dve.wait_ge(mid_loaded, t * 16 + 16)
                for j in range(TT):
                    dve.tensor_scalar(mid[:, j, :], mid[:, j, :], rms[:, bass.ds(t * TT + j, 1)], None,
                                      ALU.mult).then_inc(normed, 1)

            def turn_rest(t):
                for j in range(TT):
                    dve.wait_ge(turn_hi, t * TT + j + 1)
                    dve.tensor_tensor(hT[1][:, :, j * P:(j + 1) * P], bank_d[j][:, :].rearrange("p (c t) -> p c t", c=HC),
                                      hT[0][:, :, j * P:(j + 1) * P].bitcast(F32), ALU.subtract).then_inc(turn_lo, 1)

            def split(t, f):
                dve.wait_ge(gelu_done, t * FB + f + 1)
                if f >= 2:
                    dve.wait_ge(down_done, t * (FB - 1) + f - 1)
                else:
                    dve.wait_ge(out_filled, t * TT)
                dve.tensor_copy(g_s[0][:, f % 2, :], g[:, f % 2, :]).then_inc(g_rounded, 1)
                dve.wait_ge(g_rounded, t * FB + f + 1)
                dve.tensor_tensor(g_s[1][:, f % 2, :], g[:, f % 2, :], g_s[0][:, f % 2, :].bitcast(F32),
                                  ALU.subtract).then_inc(g_ready, 1)

            def tile(t, more):
                for f in range(FB):
                    split(t, f)
                    if f == FB // 2 and more:
                        norm(t + 1)
                if more:
                    turn_rest(t + 1)
                dve.wait_ge(res_ready, t + 1)
                for j in range(TT):
                    dve.wait_ge(out_filled, t * TT + j + 1)
                    dve.tensor_tensor(res[:, j, :], bank_o[j][:, :], res[:, j, :], ALU.add).then_inc(out_ready, 1)

            norm(0)
            turn_rest(0)
            with dve.Fori(0, TILES - 1) as t:
                tile(t, True)
            tile(TILES - 1, False)

        @block.gpsimd
        def _(pool):
            with pool.Fori(0, TILES) as t:
                pool.wait_ge(res_loaded, t * 16 + 16)
                for j in range(TT):
                    ins = pool.tensor_tensor(res[:, j, :], res[:, j, :], b2_row[:, :], ALU.add)
                ins.then_inc(res_ready, 1)


def kernel(x, ctx_2048, mask_BxS2_ik0, L0_xattn_Wq, L0_xattn_bq, L0_xattn_Wk, L0_xattn_bk, L0_xattn_Wv,
           L0_xattn_bv, L1_xattn_q_w, L1_xattn_q_b, L1_xattn_kv_w, L1_xattn_kv_b, L1_xattn_out_w,
           L1_xattn_out_b, L1_xattn_postnorm_w, L1_xattn_mlp_w1, L1_xattn_mlp_b1, L1_xattn_mlp_w2,
           L1_xattn_mlp_b2):
    import concourse.bacc as bacc
    from concourse.bass_utils import run_bass_kernel_spmd

    def stacked(a):
        return np.tile(np.asarray(a).T, (1, 3))

    def by_quarter(a):
        a = np.asarray(a)
        a = a.reshape(*a.shape[:-1], QUARTERS, HQ, D, 2)
        return np.moveaxis(a, -1, -3).reshape(*a.shape[:-4], 2 * N)

    def columns(a, n):
        return np.asarray(a).reshape(n, P).T

    arrays = dict(
        x=x, ctx_in=ctx_2048, mask=np.asarray(mask_BxS2_ik0).reshape(B, QB, P).transpose(0, 2, 1),
        wq3=stacked(L0_xattn_Wq), bq3=np.tile(np.asarray(L0_xattn_bq), 3).reshape(3 * D, 1),
        wk3=stacked(L0_xattn_Wk), bk3=np.tile(np.asarray(L0_xattn_bk), 3).reshape(3 * D, 1),
        wvT=np.asarray(L0_xattn_Wv).T, bv=columns(L0_xattn_bv, QB),
        q_w=L1_xattn_q_w, q_b=L1_xattn_q_b, kv_w=by_quarter(L1_xattn_kv_w), kv_b=by_quarter(L1_xattn_kv_b),
        out_w=L1_xattn_out_w, out_b=L1_xattn_out_b, post_w=columns(L1_xattn_postnorm_w, HC),
        w1=L1_xattn_mlp_w1, b1=columns(L1_xattn_mlp_b1, FB), w2=L1_xattn_mlp_w2, b2=L1_xattn_mlp_b2,
        ident=np.eye(P, dtype=np.float32))
    arrays = {f"in_{k}": np.ascontiguousarray(v) for k, v in arrays.items()}
    nc = bacc.Bacc("TRN2", target_bir_lowering=False, num_devices=1)
    args = [nc.dram_tensor(k, v.shape, mybir.dt.from_np(v.dtype), kind="ExternalInput").ap() for k, v in arrays.items()]
    result = nc.dram_tensor("result", (B * C, N), F32, kind="ExternalOutput").ap()
    build(nc, *args, result)
    r = run_bass_kernel_spmd(nc, [arrays], core_ids=[0])
    return r.results[0]["result"].reshape(B, C, N)
```

```python
from contextlib import ExitStack

import numpy as np
import concourse.bass as bass
from concourse import mybir

F32 = mybir.dt.float32
F32R = mybir.dt.float32r
F16 = mybir.dt.float16
BF16 = mybir.dt.bfloat16
I32 = mybir.dt.int32
ALU = mybir.AluOpType
ACT = mybir.ActivationFunctionType
AX = mybir.AxisListType

P = 128
B, C, N = 16, 256, 512
H, D = 16, 32
HQ = 4
QUARTERS = H // HQ
HC = N // P
TB = 2 * C // P
QB = C // P
SW = 3 * D + 1
VW = 3 * D
UNITS = H * QB
MASKED = -float(2 ** 126)
F = 4 * N
FB = F // P
GROUP, RING = 2, 3
GROUPS = FB // GROUP
TILES = B * C // N
TT = N // P
EPS = 1e-6

FILL = {s: [] for s in range(UNITS)}
FILL[0] = ["Ks02", "split0", "Ks03", "Qs6"]
FILL[1] = ["Qs7", "split1", "<KV10", "zq"]
FILL[2] = ["KV10", "res"]
FILL[3] = ["zk", "<KV11"]
FILL[4] = ["KV11", "aT0"]
FILL[5] = ["V10", "aT1"]
FILL[6] = ["Ks10", "Ks11", "o0"]
FILL[7] = ["Ks12", "Ks13", "o1"]
FILL[8] = ["<KV20", "zv0", "V11"]
FILL[9] = ["KV20"]
FILL[10] = ["zv1"]
FILL[11] = ["<KV21", "zS0", "KV21"]
FILL[12] = ["n0", "V20", "zS1"]
FILL[13] = ["n1", "Ks20", "Ks21", "zT0", "V21"]
FILL[14] = ["Ks22", "Ks23", "zT1"]
FILL[15] = ["<KV30", "zA0"]
FILL[16] = ["KV30"]
FILL[17] = ["zS2", "<KV31"]
FILL[18] = ["zS3", "n2", "KV31"]
FILL[19] = ["n3", "zT2"]
FILL[20] = ["Ks30", "V30", "Ks31"]
FILL[21] = ["V31", "zT3", "Ks32", "Ks33", "cT0", "mask"]
FILL[22] = ["cT1", "zA1"]
FILL[23] = ["lT0", "lT1"]
FILL[24] = ["<Q0", "Q0", "<Q1"]
FILL[25] = ["Q1"]
FILL[26] = ["<KV00", "KV00"]
FILL[27] = ["Qs0", "<KV01"]
FILL[28] = ["KV01"]
FILL[29] = ["V00", "Qs1", "Qs2", "Qs3"]
FILL[30] = ["Qs4", "Ks00", "V01"]
FILL[31] = ["Qs5", "Ks01"]
ORDER = [name for s in range(UNITS) for name in FILL[s]]
OUT = {"aT0", "aT1", "o0", "o1", "<o0", "<o1"}
PREV = OUT | {"res"}
NEXT = {n for n in ORDER if n.strip("<") in ("mask", "split0", "split1", "Q0", "Q1", "Ks00", "Ks01") or
        n.strip("<")[0] in "zncl" or n.strip("<")[:-1] in ("KV0", "V0") or (n[:2] == "Qs" and int(n[2]) < 6)}

Z_USES = [n for n in ORDER if n[0] in "zao"]
Z_V = [n for n in Z_USES if n[1] != "S"]
Z_HI = [n for n in Z_USES if n[0] == "a" or n[:2] in ("zq", "zk", "zv", "zT")]

ON_SCALAR = {"Ks01", "Ks10", "Ks11", "Ks13", "Ks20", "Ks23", "Ks30", "Ks33", "Qs0", "Qs3", "Qs4", "Qs5", "Qs7"}
P_USES = [(n, "A" if n in ON_SCALAR else "V")
          for part in (True, False) for n in ORDER if n[0] in "clQK" and (n in NEXT) == part]
P_N = len(P_USES)
P_IDX = {name: i for i, (name, _) in enumerate(P_USES)}
P_DRAINER = dict(P_USES)
P_DRAINS = {e: [name for name, d in P_USES if d == e] for e in "VA"}
P_HI = ["cT0", "cT1", "lT0", "lT1"]
TMPS = [n for n, _ in P_USES if n in ("Q0", "Q1") or n[:2] == "KV"]
WEIGHTS_BEFORE = ["zS2", "zT2", "cT0"]
LAST_STEP = 10


def upto(names, name):
    return names.index(name) + 1


def after(engine, semaphore, value):
    if not isinstance(value, int) or value > 0:
        engine.wait_ge(semaphore, value)


def load_small(nc, wts, consts, rest, early):
    with ExitStack() as ctx:
        stages = [ctx.enter_context(nc.sbuf_tensor(f"stage{i}", list(hi.shape), F32))
                  for i, (hi, lo, src) in enumerate(wts)]
        raw_loaded = [ctx.enter_context(nc.semaphore(f"raw_loaded{i}")) for i in range(len(wts))]
        consts_loaded = ctx.enter_context(nc.semaphore("consts_loaded_a"))
        hi_ready = ctx.enter_context(nc.semaphore("w_hi_ready"))
        lo_ready = ctx.enter_context(nc.semaphore("w_lo_ready"))
        with nc.Block() as block:
            @block.sync
            def _(sp):
                for st, (hi, lo, src), s in zip(stages, wts, raw_loaded):
                    sp.dma_start(st[:], src).then_inc(s, 16)
                for dst, src in consts:
                    sp.dma_start(dst, src).then_inc(consts_loaded, 16)
                early(sp)

            @block.scalar
            def _(act):
                for i, (st, (hi, lo, src)) in enumerate(zip(stages, wts)):
                    act.wait_ge(raw_loaded[i], 16)
                    act.activation(hi[:], st[:], ACT.Copy).then_inc(hi_ready, 1)

            @block.vector
            def _(dve):
                for i, (st, (hi, lo, src)) in enumerate(zip(stages, wts)):
                    dve.wait_ge(hi_ready, i + 1)
                    dve.tensor_tensor(lo[:], st[:], hi[:].bitcast(F32), ALU.subtract).then_inc(lo_ready, 1)
                rest(dve, consts_loaded, 16 * len(consts))
                dve.wait_ge(lo_ready, len(wts))


def build(nc, x, ctx_in, mask, wq3, bq3, wk3, bk3, wvT, bv, q_w, q_b, kv_w, kv_b, out_w, out_b,
          post_w, w1, b1, w2, b2, ident, out):
    lat_dram = nc.dram_tensor("lat_scratch", [B * C, N], F32, kind="Internal").ap()
    mid_dram = nc.dram_tensor("mid_scratch", [B * C, N], F32, kind="Internal").ap()
    with ExitStack() as both:
        ssq = both.enter_context(nc.sbuf_tensor("ssq", [P, B * QB], F32))
        rms = both.enter_context(nc.sbuf_tensor("rms", [P, B * QB], F32))
        idn = both.enter_context(nc.sbuf_tensor("idn", [P, P], F32))
        stage_a(nc, x, ctx_in, mask, wq3, bq3, wk3, bk3, wvT, bv, q_w, q_b, kv_w, kv_b, out_w, out_b,
                ident, lat_dram, mid_dram, ssq, idn)
        stage_b(nc, post_w, w1, b1, w2, b2, lat_dram, mid_dram, ssq, rms, idn, out)


def stage_a(nc, x, ctx_in, mask, wq3, bq3, wk3, bk3, wvT, bv, q_w, q_b, kv_w, kv_b, out_w, out_b,
            ident, lat_dram, mid_dram, ssq, idn):
    with ExitStack() as ctx:
        def sb(name, shape, dt=F32):
            return ctx.enter_context(nc.sbuf_tensor(name, shape, dt))

        def sem(name):
            return ctx.enter_context(nc.semaphore(name))

        def pair(name, shape):
            return sb(name + "_hi", shape, F32R), sb(name + "_lo", shape, F32R)

        wq_t, wk_t, wv_t = pair("wq_t", [P, QB, 3 * D]), pair("wk_t", [P, QB, 3 * D]), pair("wv_t", [P, QB, C])
        qw, kvw, ow = pair("qw", [P, HC, N]), pair("kvw", [P, HC, 2 * N]), pair("ow", [P, HC, N])
        idr = sb("idr", [P, P], F32R)
        bq = sb("bq", [3 * D, 1])
        bk = sb("bk", [3 * D, 1])
        bvc = sb("bvc", [P, QB])
        qb_row = sb("qb_row", [P, N])
        kvb_row = sb("kvb_row", [P, 2 * N])
        ob_row = sb("ob_row", [P, N])

        def chunks(w):
            return w.rearrange("(c p) m -> p c m", p=P)

        ones_col = sb("ones_col", [P, 1])
        ready = sem("setup_done")

        def rest(dve, sem_, value):
            dve.memset(ones_col[:], 1.0).then_inc(ready, 1)
            dve.wait_ge(sem_, value)
            dve.tensor_copy(idr[:], idn[:]).then_inc(ready, 1)
            dve.tensor_scalar(qb_row[:], qb_row[:], 1.0 / D, None, ALU.mult).then_inc(ready, 1)
            dve.wait_ge(ready, 3)

        x_raw = sb("x_raw", [P, QB, N])
        ctx_raw = sb("ctx_raw", [P, QB, N])
        mask_raw = sb("mask_raw", [P, QB], I32)
        mask_bias = sb("mask_bias", [P, TB])
        loaded, w_loaded = sem("inputs_loaded"), [sem(f"w_loaded{i}") for i in range(3)]
        w_hi, w_lo = sem("w_hi_a"), sem("w_lo_a")

        def load(sp, b):
            sp.dma_start(ctx_raw[:], ctx_in[b].rearrange("(t p) n -> p t n", p=P)).then_inc(loaded, 16)
            sp.dma_start(x_raw[:], x[b].rearrange("(t p) n -> p t n", p=P)).then_inc(loaded, 16)
            sp.dma_start(mask_raw[:], mask[b]).then_inc(loaded, 16)

        with nc.sbuf_tensor("w_raw", [P, HC, 4 * N], F32) as w_raw:
            big = [(w_raw[:, :, 0:N], qw, q_w, 1.0 / D), (w_raw[:, :, N:3 * N], kvw, kv_w, 1.0),
                   (w_raw[:, :, 3 * N:4 * N], ow, out_w, 1.0)]

            def early(sp):
                load(sp, 0)
                for (raw, parts, src, scale), s in zip(big, w_loaded):
                    sp.dma_start(raw, chunks(src)).then_inc(s, 16)

            load_small(nc, [(*wq_t, chunks(wq3)), (*wk_t, chunks(wk3)), (*wv_t, chunks(wvT))],
                       [(idn[:], ident), (bq[:], bq3), (bk[:], bk3), (bvc[:], bv),
                        (qb_row[:], q_b.partition_broadcast(P)), (kvb_row[:], kv_b.partition_broadcast(P)),
                        (ob_row[:], out_b.partition_broadcast(P))], rest, early)
        hT = pair("hT", [P, HC, TB * P])
        q_stack = sb("q_stack", [SW, H, C], F32R)
        turn = pair("turn", [P, QB * N])
        x_s = [t[:, :].rearrange("p (c n) -> p c n", c=QB) for t in turn]
        vT_s = [t[:, :].rearrange("p (m c) -> p m c", m=HC) for t in turn]
        aT_s = [t[:, :].rearrange("p (c q) -> p c q", c=HC) for t in turn]
        ctx_s = pair("ctx_s", [P, QB, N])
        p0 = sb("p0", [P, 2, N])
        q_region = sb("q_region", [P, QB * H * SW], F32R)
        q_tok = q_region[:, :].rearrange("p (q h s) -> p q h s", q=QB, h=H)
        q0_stack = q_region[0:3 * D, 0:N]
        k0_stack = q_region[0:3 * D, N:2 * N]
        pT0 = [q_region[:, 2 * N + i * HC * 256:2 * N + (i + 1) * HC * 256].rearrange("p (m n) -> p m n", m=HC)
               for i in range(2)]
        assert 2 * N + 2 * HC * 256 <= QB * H * SW
        lat = sb("lat", [P, QB, N])
        lat_b = sb("lat_b", [P, QB, N])
        k_tok = sb("k_tok", [P, TB, HQ, SW], F32R)
        k_stack = sb("k_stack", [SW, 2, HQ, TB * P], F32R)
        tmp = sb("tmp", [P, 2, N])
        vs = sb("vs", [P, 2, TB, HQ, VW], BF16)
        prob = sb("prob", [P, 2, TB * P])
        pT_hi = sb("pT_hi", [P, 2, TB, P], F16)
        pT_lo = sb("pT_lo", [P, 2, TB, P], F16)
        attn = sb("attn", [P, QB, N])
        o_sum = sb("o_sum", [P, 4, D])
        nmax0, sum0, rec0 = sb("nmax0", [P, HC]), sb("sum0", [P, HC]), sb("rec0", [P, HC])
        nmax, sums, rec = sb("nmax", [P, UNITS]), sb("sums", [P, UNITS]), sb("rec", [P, 4])

        ps = [ctx.enter_context(nc.psum_tensor(f"bank{i}", [P, N], F32)) for i in range(8)]
        bank_s, bank_t, bank_p, bank_o, bank_0 = ps[0:2], ps[2:4], ps[4:6], ps[6], ps[7]

        split_hi, split_lo = sem("split_hi"), sem("split_lo")
        z_filled, z_hi, z_drained = sem("z_filled"), sem("z_hi"), sem("z_drained_v")
        l0_max, l0_exp, l0_rec, l0_norm = sem("l0_max"), sem("l0_exp"), sem("l0_rec"), sem("l0_norm")
        lat_stored, lat_b_ready, mask_ready = sem("lat_stored"), sem("lat_b_ready"), sem("mask_ready")
        p_filled, p_hi = sem("p_filled"), sem("p_hi")
        p_drained = {"V": sem("p_drained_v"), "A": sem("p_drained_a")}
        tmp_hi, vals_hi, stacked, tmp_used, g_step = (sem("tmp_hi"), sem("vals_hi"), sem("stacked"), sem("tmp_used"),
                                                      sem("g_step"))
        s_filled, s_max, s_exp = sem("s_filled"), sem("s_max"), sem("s_exp")
        t_filled, t_hi, t_lo = sem("t_filled"), sem("t_hi"), sem("t_lo")
        av_filled, o_summed, o_ready = sem("av_filled"), sem("o_summed"), sem("o_ready")
        res_loaded = sem("res_loaded_a")
        mid_stored, squared, g_rec, zero_ready = sem("mid_stored"), sem("squared"), sem("g_rec"), sem("zero_ready")

        SPLIT3 = ((0, 0), (1, 0), (0, 1))

        def z_at(it, prev, more, uses, name):
            def n(p, m):
                return sum(u in PREV for u in uses) * p + sum(u not in PREV for u in uses) * m
            if isinstance(it, int):
                base = sum(n(i > 0, i < B - 1) for i in range(-1, it))
            else:
                base = n(0, 1) * 2 + (it - 1) * n(1, 1)
            live = [u for u in uses if (prev if u in PREV else more)]
            return base + (upto(live, name) if name else 0)

        def p_at(b, name):
            return b * P_N + P_IDX[name] + 1

        def p_dr(b, name):
            d = P_DRAINER[name]
            return p_drained[d], b * len(P_DRAINS[d]) + upto(P_DRAINS[d], name)

        def p_bank(name):
            return bank_p[P_IDX[name] % 2]

        assert not any(n in Z_V + P_HI + TMPS + ["o0", "o1"] for n in FILL[UNITS - 1])

        def run(engine, step, fill, late=(), rest=None, split_weights=None):
            def fills(names, b, prev, cur, more):
                for name in names:
                    if name in PREV and prev:
                        fill(name, b - 1, b, prev, more)
                    elif name in NEXT and more:
                        fill(name, b + 1, b, prev, more)
                    elif name not in PREV and name not in NEXT and cur:
                        fill(name, b, b, prev, more)

            def iteration(b, prev, cur, more, steps=UNITS):
                for s in range(steps):
                    step(b, s, prev, cur, more)
                    if s > 0:
                        fills([n for n in FILL[s - 1] if n in late], b, prev, cur, more)
                    if rest:
                        rest(b, s, prev, cur, more)
                    fills([n for n in FILL[s] if n not in late], b, prev, cur, more)

            for name in ORDER:
                if name in WEIGHTS_BEFORE and split_weights:
                    split_weights(WEIGHTS_BEFORE.index(name))
                if name in NEXT:
                    fills([name], -1, False, False, True)
            iteration(0, False, True, True)
            with engine.Fori(1, B - 1) as b:
                iteration(b, True, True, True)
            iteration(B - 1, True, True, False)
            iteration(B, True, False, False, LAST_STEP)

        block = ctx.enter_context(nc.Block())

        @block.sync
        def _(sp):
            def store_latents(n, it, prev):
                sp.wait_ge(z_drained, z_at(it, prev, True, Z_V, "zA1"))
                sp.dma_start(lat_dram.rearrange("(b t p) n -> b p t n", p=P, t=QB)[n], lat[:]).then_inc(lat_stored, 16)

            def residual(n):
                sp.wait_ge(lat_stored, 16 * n + 16)
                after(sp, squared, 16 * n)
                after(sp, mid_stored, 16 * n)
                sp.dma_start(lat_b[:], lat_dram.rearrange("(b t p) n -> b p t n", p=P, t=QB)[n]).then_inc(res_loaded, 16)

            def store_mid(n, it, more):
                sp.wait_ge(z_drained, z_at(it, True, more, Z_V, "o1"))
                sp.dma_start(mid_dram.rearrange("(b t p) n -> b p t n", p=P, t=QB)[n], lat_b[:]).then_inc(mid_stored, 16)

            def load_next(n):
                sp.wait_ge(p_filled, p_at(n - 1, "lT0"))
                load(sp, n)

            store_latents(0, -1, False)
            load_next(1)
            store_latents(1, 0, False)
            load_next(2)
            with sp.Fori(1, B - 2) as b:
                residual(b - 1)
                store_mid(b - 1, b, True)
                store_latents(b + 1, b, True)
                load_next(b + 2)
            residual(B - 3)
            store_mid(B - 3, B - 2, True)
            store_latents(B - 1, B - 2, True)
            residual(B - 2)
            store_mid(B - 2, B - 1, False)
            residual(B - 1)
            store_mid(B - 1, B, False)
            sp.wait_ge(lat_stored, 16 * B)
            sp.wait_ge(mid_stored, 16 * B)

        @block.tensor
        def _(pe):
            def halves(name):
                return (0,) if name[0] == "<" else (1,) if "<" + name in ORDER else (0, 1)

            def z_free(n, it, prev, more, name):
                last = ([u for u in Z_USES[:Z_USES.index(name.strip("<"))] if (prev if u in PREV else more)] or [""])[-1]
                if last[1:2] == "S":
                    pe.wait_ge(l0_exp, n * HC + int(last[2]) + 1)
                else:
                    after(pe, z_drained, z_at(it, prev, more, Z_V, last))

            def l0_project(w, src):
                for i, (wp, mp) in enumerate(SPLIT3):
                    for c in range(QB):
                        mm = pe.matmul(bank_0[0:3 * D, :], w[wp][:, c, :], src[mp][:, c, :],
                                       start=(i == 0 and c == 0), stop=(i == 2 and c == QB - 1))
                return mm

            def l0_values(j):
                for t in range(2):
                    m = 2 * j + t
                    for i, (wp, mp) in enumerate(SPLIT3):
                        for c in range(QB):
                            mm = pe.matmul(bank_0[:, t * C:(t + 1) * C], ctx_s[mp][:, c, m * P:(m + 1) * P],
                                           wv_t[wp][:, c, :], start=(i == 0 and c == 0),
                                           stop=(i == 2 and c == QB - 1))
                return mm

            def l0_scores(nb):
                return pe.matmul(bank_0[:, :], q0_stack[:, nb * P:(nb + 1) * P], k0_stack[:, :],
                                 start=True, stop=True)

            def l0_turn(nb):
                for m in range(HC):
                    mm = pe.transpose(bank_0[:, m * P:(m + 1) * P], p0[:, nb % 2, m * P:(m + 1) * P], idn[:])
                return mm

            def l0_out(blocks):
                for cb in blocks:
                    for i, (wp, mp) in enumerate(SPLIT3):
                        for m in range(HC):
                            mm = pe.matmul(bank_0[:, cb * C:(cb + 1) * C], vT_s[wp][:, m, cb * P:(cb + 1) * P],
                                           pT0[mp][:, m, :], start=(i == 0 and m == 0),
                                           stop=(i == 2 and m == HC - 1))
                return mm

            def l0(n, it, prev, more, name):
                blocks = halves(name)
                if 0 in blocks:
                    z_free(n, it, prev, more, name)
                name = name.strip("<")
                kind, j = name[1], int(name[2:] or 0)
                if kind in "qk":
                    pe.wait_ge(split_lo, n * 2 + 1 + (kind == "k"))
                    mm = l0_project(wq_t, x_s) if kind == "q" else l0_project(wk_t, ctx_s)
                elif kind == "v":
                    mm = l0_values(j)
                elif kind == "S":
                    mm = l0_scores(j)
                elif kind == "T":
                    pe.wait_ge(l0_norm, n * HC + j + 1)
                    mm = l0_turn(j)
                else:
                    mm = l0_out(blocks)
                if 1 in blocks:
                    mm.then_inc(z_filled, 1)

            def p_free(b, name):
                i = P_IDX[name]
                if i < 2:
                    last, d = P_USES[i - 2]
                    after(pe, p_drained[d], (b - 1) * len(P_DRAINS[d]) + upto(P_DRAINS[d], last))
                else:
                    pe.wait_ge(*p_dr(b, P_USES[i - 2][0]))

            def turn(bank, src, blk):
                for hc in range(HC):
                    mm = pe.transpose(bank[:, hc * P:(hc + 1) * P], src[:, blk, hc * P:(hc + 1) * P], idn[:])
                return mm

            def project(bank, o, src, t, w, first):
                for i, (wp, mp) in enumerate(SPLIT3):
                    for hc in range(HC):
                        mm = pe.matmul(bank[:, o * 256:(o + 1) * 256], src[mp][:, hc, t * P:(t + 1) * P],
                                       w[wp][:, hc, first:first + 256], start=(i == 0 and hc == 0),
                                       stop=(i == 2 and hc == HC - 1))
                return mm

            def l1_fill(b, it, prev, more, name):
                blocks, name = halves(name), name.strip("<")
                bank = p_bank(name)
                if 0 in blocks:
                    p_free(b, name)
                if name[1] == "T":
                    if name == "lT0":
                        pe.wait_ge(z_drained, z_at(it, prev, more, Z_V, "zA1"))
                    mm = turn(bank, ctx_raw if name[0] == "c" else lat, int(name[2]))
                elif name in ("Q0", "Q1"):
                    if name == "Q0" and 0 in blocks:
                        pe.wait_ge(*p_dr(b, "lT1"))
                    for o in blocks:
                        mm = project(bank, o, hT, 2 + int(name[1]), qw, o * 256)
                elif name[:2] == "Qs":
                    i = int(name[2])
                    if i == 0:
                        pe.wait_ge(stacked, b * len(TMPS) + 2)
                    for j in range(4):
                        mm = pe.transpose(bank[0:SW, j * P:(j + 1) * P].bitcast(F32R),
                                          q_tok[:, j % 2, 2 * i + j // 2, :], idr[:])
                elif name[:2] == "KV":
                    q, half = int(name[2]), int(name[3])
                    for o in blocks:
                        mm = project(bank, o, hT, 2 * half + o, kvw, q * 256)
                else:
                    q, i = int(name[2]), int(name[3])
                    if i == 0:
                        pe.wait_ge(stacked, b * len(TMPS) + upto(TMPS, f"KV{q}1"))
                    for t in range(TB):
                        mm = pe.transpose(bank[0:SW, t * P:(t + 1) * P].bitcast(F32R), k_tok[:, t, i, :], idr[:])
                if 1 in blocks:
                    mm.then_inc(p_filled, 1)

            def out(b, it, prev, more, name):
                blocks = halves(name)
                if 0 in blocks:
                    z_free(b, it, prev, more, name)
                qb = int(name[-1])
                if name == "aT0":
                    pe.wait_ge(o_ready, b * (UNITS // 4) + UNITS // 4)
                if name[0] == "a":
                    mm = turn(bank_0, attn, qb)
                else:
                    for o in blocks:
                        mm = project(bank_0, o, aT_s, qb, ow, o * 256)
                if 1 in blocks:
                    mm.then_inc(z_filled, 1)

            def scores(b, u):
                h, qb = u // QB, u % QB
                after(pe, s_exp, b * UNITS + u - 1)
                if u % 2 == 0:
                    pe.wait_ge(*p_dr(b, f"Ks{h // HQ}{h % HQ}"))
                pe.matmul(bank_s[u % 2][:, :], q_stack[:, h, qb * P:(qb + 1) * P],
                          k_stack[:, (h // HQ) % 2, h % HQ, :], start=True, stop=True).then_inc(s_filled, 1)

            def probs_turn(b, u):
                pe.wait_ge(s_exp, b * UNITS + u + 1)
                after(pe, t_lo, b * UNITS + u - 1)
                for t in range(TB):
                    mm = pe.transpose(bank_t[u % 2][:, t * P:(t + 1) * P], prob[:, u % 2, t * P:(t + 1) * P], idn[:])
                mm.then_inc(t_filled, 1)

            def weigh(b, u):
                h = u % UNITS // QB
                pe.wait_ge(t_lo, b * UNITS + u + 1)
                if u % 4 == 0:
                    after(pe, o_summed, b * (UNITS // 4) + u // 4)
                if u % (2 * HQ) == 0:
                    pe.wait_ge(tmp_used, b * len(TMPS) + upto(TMPS, f"KV{h // HQ}1"))
                o = (u % 4) * VW
                v = vs[:, (h // HQ) % 2, :, h % HQ, :]
                pe.matmul(bank_o[:, o:o + VW], pT_hi[:, u % 2, 0, :], v[:, 0, :], start=True, stop=False)
                for t in range(TB):
                    pe.matmul(bank_o[:, o:o + 2 * D], pT_lo[:, u % 2, t, :], v[:, t, 0:2 * D], start=False, stop=False)
                for t in range(1, TB):
                    mm = pe.matmul(bank_o[:, o:o + VW], pT_hi[:, u % 2, t, :], v[:, t, :],
                                   start=False, stop=(t == TB - 1))
                mm.then_inc(av_filled, 1)

            def step(b, s, prev, cur, more):
                if cur:
                    scores(b, s)
                if cur if s >= 4 else prev:
                    weigh(b, s - 4)
                if cur if s >= 2 else prev:
                    probs_turn(b, s - 2)

            def fill(name, b, it, prev, more):
                if name in OUT:
                    out(b, it, prev, more, name)
                elif name.strip("<") in Z_USES:
                    l0(b, it, prev, more, name)
                elif name.strip("<") in P_IDX:
                    l1_fill(b, it, prev, more, name)

            run(pe, step, fill)

        @block.scalar
        def _(act):
            def split(n, i):
                act.wait_ge(loaded, n * 48 + 48)
                hi, raw = ((x_s[0], x_raw[:]), (ctx_s[0][:], ctx_raw[:]))[i]
                act.activation(hi, raw, ACT.Copy).then_inc(split_hi, 1)

            def l0(n, it, prev, more, name):
                kind, j = name[1], int(name[2:] or 0)
                if kind == "S":
                    act.wait_ge(l0_max, n * HC + j + 1)
                    act.activation(p0[:, j % 2, :], bank_0[:, :], ACT.Exp, bias=nmax0[:, j:j + 1],
                                   accum_out=sum0[:, j:j + 1]).then_inc(l0_exp, 1)
                elif kind != "A":
                    act.wait_ge(z_filled, z_at(it, prev, more, Z_USES, name))
                    if kind == "q":
                        ins = act.activation(q0_stack, bank_0[0:3 * D, :], ACT.Identity, bias=bq[:, 0:1])
                    elif kind == "k":
                        ins = act.activation(k0_stack, bank_0[0:3 * D, :], ACT.Identity, bias=bk[:, 0:1])
                    elif kind == "v":
                        ins = act.activation(vT_s[0][:, 2 * j:2 * j + 2, :],
                                             bank_0[:, :].rearrange("p (m c) -> p m c", m=2), ACT.Copy)
                    else:
                        ins = act.activation(pT0[0][:, :, j % 2 * P:(j % 2 + 1) * P],
                                             bank_0[:, :].rearrange("p (m n) -> p m n", m=HC), ACT.Copy)
                    ins.then_inc(z_hi, 1)

            def l1_fill(b, name):
                if name in P_HI:
                    t = P_HI.index(name)
                    act.wait_ge(p_filled, p_at(b, name))
                    act.activation(hT[0][:, :, t * P:(t + 1) * P],
                                   p_bank(name)[:, :].rearrange("p (c t) -> p c t", c=HC), ACT.Copy).then_inc(p_hi, 1)
                elif name in ("Q0", "Q1"):
                    qb = int(name[1])
                    act.wait_ge(*p_dr(b, name))
                    src = tmp[:, qb, :].rearrange("p (h d) -> p h d", d=D)
                    for part in range(2):
                        ins = act.activation(q_tok[:, qb, :, part * D:(part + 1) * D], src, ACT.Copy)
                    ins.then_inc(tmp_hi, 1)
                elif name[:2] == "KV":
                    q, half = int(name[2]), int(name[3])
                    k = TMPS.index(name)
                    act.wait_ge(*p_dr(b, name))
                    src = tmp[:, k % 2, 0:256].rearrange("p (a d) -> p a d", d=D)
                    dst = k_tok[:, 2 * half:2 * half + 2, :, :].rearrange("p t h s -> p (t h) s")
                    act.activation(dst[:, :, 0:D], src, ACT.Copy)
                    act.activation(dst[:, :, 2 * D:3 * D], src, ACT.Copy).then_inc(tmp_hi, 1)
                elif P_DRAINER[name] == "A":
                    act.wait_ge(p_filled, p_at(b, name))
                    src = p_bank(name)[0:SW, :]
                    if name[0] == "Q":
                        i = int(name[2])
                        ins = act.activation(q_stack[:, 2 * i:2 * i + 2, :], src.rearrange("p (h q) -> p h q", h=2), ACT.Copy)
                    else:
                        ins = act.activation(k_stack[:, int(name[2]) % 2, int(name[3]), :], src, ACT.Copy)
                    ins.then_inc(p_drained["A"], 1)

            def values(b, name):
                q, half = int(name[1]), int(name[2])
                k = TMPS.index("K" + name)
                after(act, av_filled, b * UNITS + (q - 1) * 2 * HQ)
                act.activation(vs[:, q % 2, 2 * half:2 * half + 2, :, 0:D].rearrange("p t h s -> p (t h) s"),
                               tmp[:, k % 2, 256:512].rearrange("p (a d) -> p a d", d=D),
                               ACT.Copy).then_inc(vals_hi, 1)

            def out(b, it, more, name):
                qb = int(name[-1])
                if name[0] == "a":
                    act.wait_ge(z_filled, z_at(it, True, more, Z_USES, name))
                    act.activation(aT_s[0][:, :, qb * P:(qb + 1) * P], bank_0[:, :].rearrange("p (c t) -> p c t", c=HC),
                                   ACT.Copy).then_inc(z_hi, 1)
                else:
                    act.wait_ge(z_drained, z_at(it, True, more, Z_V, name))
                    act.activation(p0[:, qb, :], lat_b[:, qb, :], ACT.Square,
                                   accum_out=ssq[:, bass.ds(b * QB + qb, 1)]).then_inc(squared, 8)

            def soft(b, u):
                act.wait_ge(s_max, b * UNITS + u + 1)
                after(act, t_filled, b * UNITS + u - 1)
                act.activation(prob[:, u % 2, :], bank_s[u % 2][:, :], ACT.Exp, bias=nmax[:, u:u + 1],
                               accum_out=sums[:, u:u + 1]).then_inc(s_exp, 1)

            def prob_round(b, u):
                act.wait_ge(t_filled, b * UNITS + u + 1)
                after(act, av_filled, b * UNITS + u - 1)
                act.activation(pT_hi[:, u % 2, :, :], bank_t[u % 2][:, :].rearrange("p (t q) -> p t q", t=TB),
                               ACT.Copy).then_inc(t_hi, 1)

            def step(b, s, prev, cur, more):
                if cur if s >= 3 else prev:
                    prob_round(b, s - 3)
                if cur:
                    soft(b, s)

            def fill(name, b, it, prev, more):
                if name[:5] == "split":
                    split(b, int(name[5]))
                elif name in OUT and name in Z_USES:
                    out(b, it, more, name)
                elif name in Z_USES:
                    l0(b, it, prev, more, name)
                elif name[0] == "V":
                    values(b, name)
                elif name in P_IDX:
                    l1_fill(b, name)

            def split_weights(i):
                raw, parts, src, scale = big[i]
                act.wait_ge(w_loaded[i], 16)
                act.activation(parts[0][:], raw, ACT.Copy, scale=scale).then_inc(w_hi, 1)
                if i == len(big) - 1:
                    act.wait_ge(w_lo, len(big))

            run(act, step, fill, TMPS + ["o0", "o1"], None, split_weights)

        @block.vector
        def _(dve):
            def mask_to_bias(n):
                dve.wait_ge(loaded, n * 48 + 48)
                after(dve, stacked, n * len(TMPS))
                dve.tensor_scalar(mask_bias[:, 0:QB], mask_raw[:, :], 0.0, MASKED, ALU.is_equal,
                                  ALU.mult).then_inc(mask_ready, 1)

            def stack_rest(stack, rows, bias):
                return dve.scalar_tensor_tensor(out=stack[rows, :], in0=bank_0[rows, :], scalar=bias[rows, 0:1],
                                                in1=stack[rows, :].bitcast(F32), op0=ALU.add, op1=ALU.subtract)

            def l0(n, it, prev, more, name):
                kind, j = name[1], int(name[2:] or 0)
                if kind == "S":
                    dve.wait_ge(z_filled, z_at(it, prev, more, Z_USES, name))
                    dve.tensor_reduce(nmax0[:, j:j + 1], bank_0[:, :], AX.X, ALU.max, negate=True).then_inc(l0_max, 1)
                    return
                if kind == "A":
                    dve.wait_ge(z_filled, z_at(it, prev, more, Z_USES, name))
                    if j == 0:
                        after(dve, lat_stored, n * 16)
                    for cb in range(QB):
                        ins = dve.scalar_tensor_tensor(
                            out=lat[:, cb, j * C:(j + 1) * C], in0=bank_0[:, cb * C:(cb + 1) * C],
                            scalar=bvc[:, cb:cb + 1], in1=x_raw[:, cb, j * C:(j + 1) * C], op0=ALU.add, op1=ALU.add)
                    ins.then_inc(z_drained, 1)
                    return
                dve.wait_ge(z_hi, z_at(it, prev, more, Z_HI, name))
                if kind == "q":
                    ins = stack_rest(q0_stack, slice(2 * D, 3 * D), bq)
                elif kind == "k":
                    ins = stack_rest(k0_stack, slice(D, 2 * D), bk)
                elif kind == "v":
                    ins = dve.tensor_tensor(vT_s[1][:, 2 * j:2 * j + 2, :], bank_0[:, :].rearrange("p (m c) -> p m c", m=2),
                                            vT_s[0][:, 2 * j:2 * j + 2, :].bitcast(F32), ALU.subtract)
                else:
                    part = slice(j % 2 * P, (j % 2 + 1) * P)
                    ins = dve.tensor_tensor(pT0[1][:, :, part], bank_0[:, :].rearrange("p (m n) -> p m n", m=HC),
                                            pT0[0][:, :, part].bitcast(F32), ALU.subtract)
                ins.then_inc(z_drained, 1)

            def reciprocal(n, nb):
                dve.wait_ge(l0_exp, n * HC + nb + 1)
                dve.reciprocal(rec0[:, nb:nb + 1], sum0[:, nb:nb + 1]).then_inc(l0_rec, 1)

            def l1_fill(b, name):
                if name in P_HI:
                    t = P_HI.index(name)
                    part = slice(t * P, (t + 1) * P)
                    dve.wait_ge(p_hi, b * len(P_HI) + t + 1)
                    dve.tensor_tensor(hT[1][:, :, part], p_bank(name)[:, :].rearrange("p (c t) -> p c t", c=HC),
                                      hT[0][:, :, part].bitcast(F32), ALU.subtract).then_inc(p_drained["V"], 1)
                elif name in TMPS:
                    k = TMPS.index(name)
                    dve.wait_ge(p_filled, p_at(b, name))
                    after(dve, tmp_used, b * len(TMPS) + k - 1)
                    if name[0] == "Q":
                        out_, in_, row = tmp[:, k % 2, :], p_bank(name)[:, :], qb_row[:, :]
                    else:
                        q = int(name[2])
                        out_ = tmp[:, k % 2, :].rearrange("p (v t e) -> p v t e", v=2, t=2)
                        in_ = p_bank(name)[:, :].rearrange("p (t v e) -> p v t e", v=2, t=2)
                        row = kvb_row[:, q * 256:(q + 1) * 256].rearrange("p (v o e) -> p v o e", v=2, o=1)
                        row = row.to_broadcast([P, 2, 2, P])
                    dve.tensor_tensor(out_, in_, row, ALU.add).then_inc(p_drained["V"], 1)
                elif P_DRAINER[name] == "V":
                    dve.wait_ge(p_filled, p_at(b, name))
                    src = p_bank(name)[0:SW, :]
                    if name[0] == "Q":
                        i = int(name[2])
                        ins = dve.tensor_copy(q_stack[:, 2 * i:2 * i + 2, :], src.rearrange("p (h q) -> p h q", h=2))
                    else:
                        ins = dve.tensor_copy(k_stack[:, int(name[2]) % 2, int(name[3]), :], src)
                    ins.then_inc(p_drained["V"], 1)

            def out(b, it, more, name):
                qb = int(name[-1])
                if name[0] == "a":
                    dve.wait_ge(z_hi, z_at(it, True, more, Z_HI, name))
                    part = slice(qb * P, (qb + 1) * P)
                    dve.tensor_tensor(aT_s[1][:, :, part], bank_0[:, :].rearrange("p (c t) -> p c t", c=HC),
                                      aT_s[0][:, :, part].bitcast(F32), ALU.subtract).then_inc(z_drained, 1)
                else:
                    dve.wait_ge(z_filled, z_at(it, True, more, Z_USES, name))
                    dve.wait_ge(lat_b_ready, b + 1)
                    dve.tensor_tensor(lat_b[:, qb, :], bank_0[:, :], lat_b[:, qb, :], ALU.add).then_inc(z_drained, 1)

            def peak(b, u):
                dve.wait_ge(s_filled, b * UNITS + u + 1)
                dve.tensor_reduce(nmax[:, u:u + 1], bank_s[u % 2][:, :], AX.X, ALU.max, negate=True).then_inc(s_max, 1)

            def prob_rest(b, u):
                dve.wait_ge(t_hi, b * UNITS + u + 1)
                dve.tensor_tensor(pT_lo[:, u % 2, :, :], bank_t[u % 2][:, :].rearrange("p (t q) -> p t q", t=TB),
                                  pT_hi[:, u % 2, :, :], ALU.subtract).then_inc(t_lo, 1)

            def heads_out(b, g, prev, more):
                n = UNITS // 4
                i = g % n
                dve.wait_ge(av_filled, b * UNITS + 4 * g + 4)
                dve.reciprocal(rec[:, :], sums[:, 4 * i:4 * i + 4]).then_inc(g_rec, 1)
                dve.tensor_reduce(o_sum[:, :, :],
                                  bank_o[:, 0:4 * VW].rearrange("p (u v d) -> p u d v", u=4, v=3),
                                  AX.X, ALU.add).then_inc(o_summed, 1)
                dve.wait_ge(g_rec, b * n + g + 1)
                dve.wait_ge(o_summed, b * n + g + 1)
                if g == 0 and prev:
                    dve.wait_ge(z_filled, z_at(b, True, more, Z_USES, "aT1"))
                for hh in range(2):
                    ins = dve.tensor_tensor(
                        attn[:, :, (2 * i + hh) * D:(2 * i + hh + 1) * D], o_sum[:, 2 * hh:2 * hh + 2, :],
                        rec[:, 2 * hh:2 * hh + 2].rearrange("p (q o) -> p q o", o=1).to_broadcast([P, 2, D]),
                        ALU.mult)
                ins.then_inc(o_ready, 1)

            def step(b, s, prev, cur, more):
                if cur:
                    peak(b, s)

            def rest(b, s, prev, cur, more):
                if cur if s >= 3 else prev:
                    prob_rest(b, s - 3)
                if s % 4 == 3 and (cur if s >= 7 else prev):
                    heads_out(b, s // 4 - 1, prev, more)

            def fill(name, b, it, prev, more):
                if name == "mask":
                    mask_to_bias(b)
                elif name[0] == "n":
                    reciprocal(b, int(name[1]))
                elif name in OUT and name in Z_USES:
                    out(b, it, more, name)
                elif name in Z_USES:
                    l0(b, it, prev, more, name)
                elif name in P_IDX:
                    l1_fill(b, name)

            def split_weights(i):
                raw, parts, src, scale = big[i]
                dve.wait_ge(w_hi, i + 1)
                dve.scalar_tensor_tensor(out=parts[1][:], in0=raw, scalar=scale, in1=parts[0][:].bitcast(F32),
                                         op0=ALU.mult, op1=ALU.subtract).then_inc(w_lo, 1)

            run(dve, step, fill, Z_V + P_HI, rest, split_weights)

        @block.gpsimd
        def _(pool):
            def stack_rest(b, name):
                k = TMPS.index(name)
                pool.wait_ge(tmp_hi, b * len(TMPS) + k + 1)
                if name[0] == "Q":
                    dst = q_tok[:, k, :, :]
                    src = tmp[:, k % 2, :].rearrange("p (h d) -> p h d", d=D)
                    pool.tensor_tensor(dst[:, :, 2 * D:3 * D], src, dst[:, :, 0:D].bitcast(F32),
                                       ALU.subtract).then_inc(tmp_used, 1)
                    pool.tensor_copy(dst[:, :, 3 * D:SW], ones_col[:, :].rearrange("p (a o) -> p a o", o=1)
                                     .to_broadcast([P, H, 1])).then_inc(stacked, 1)
                    return
                half = int(name[3])
                if name == "KV00":
                    pool.wait_ge(mask_ready, b + 1)
                src = tmp[:, k % 2, 0:256].rearrange("p (a d) -> p a d", d=D)
                dst = k_tok[:, 2 * half:2 * half + 2, :, :].rearrange("p t h s -> p (t h) s")
                pool.tensor_tensor(dst[:, :, D:2 * D], src, dst[:, :, 0:D].bitcast(F32), ALU.subtract)
                for t in range(2 * half, 2 * half + 2):
                    ins = pool.tensor_copy(k_tok[:, t, :, 3 * D:SW], mask_bias[:, t:t + 1].rearrange(
                        "p (a o) -> p a o", o=1).to_broadcast([P, HQ, 1]))
                ins.then_inc(stacked, 1)

            def values_rest(b, name):
                q, half, k = int(name[2]), int(name[3]), TMPS.index(name)
                val = tmp[:, k % 2, 256:512].rearrange("p (a d) -> p a d", d=D)
                v = vs[:, q % 2, 2 * half:2 * half + 2, :, :].rearrange("p t h s -> p (t h) s")
                n = b * (2 * QUARTERS * 2) + (k - 2) * 2
                pool.wait_ge(vals_hi, b * 2 * QUARTERS + k - 1)
                pool.tensor_tensor(v[:, :, D:2 * D], val, v[:, :, 0:D], ALU.subtract).then_inc(g_step, 1)
                pool.wait_ge(g_step, n + 1)
                pool.tensor_tensor(val, val, v[:, :, 0:D], ALU.subtract).then_inc(g_step, 1)
                pool.wait_ge(g_step, n + 2)
                pool.tensor_tensor(v[:, :, 2 * D:3 * D], val, v[:, :, D:2 * D], ALU.subtract).then_inc(tmp_used, 1)

            def split(b, i):
                hi, lo, raw = ((x_s[0], x_s[1], x_raw[:]), (ctx_s[0][:], ctx_s[1][:], ctx_raw[:]))[i]
                pool.wait_ge(split_hi, b * 2 + i + 1)
                pool.tensor_tensor(lo, raw, hi.bitcast(F32), ALU.subtract).then_inc(split_lo, 1)

            def normalise(b, nb):
                pool.wait_ge(l0_rec, b * HC + nb + 1)
                pool.tensor_tensor(p0[:, nb % 2, :], p0[:, nb % 2, :], rec0[:, nb:nb + 1].to_broadcast([P, N]),
                                   ALU.mult).then_inc(l0_norm, 1)

            def residual(b):
                pool.wait_ge(res_loaded, b * 16 + 16)
                for qb in range(QB):
                    ins = pool.tensor_tensor(lat_b[:, qb, :], lat_b[:, qb, :], ob_row[:, :], ALU.add)
                ins.then_inc(lat_b_ready, 1)

            pool.memset(mask_bias[:, QB:TB], 0.0).then_inc(zero_ready, 1)
            pool.wait_ge(zero_ready, 1)
            def step(b, s, prev, cur, more):
                pass

            def fill(name, b, it, prev, more):
                if name == "res":
                    residual(b)
                elif name[:5] == "split":
                    split(b, int(name[5]))
                elif name[0] == "n":
                    normalise(b, int(name[1]))
                elif name[0] == "V":
                    values_rest(b, "K" + name)
                elif name in TMPS:
                    stack_rest(b, name)

            run(pool, step, fill)


def stage_b(nc, post_w, w1, b1, w2, b2, lat_dram, mid_dram, ssq, rms, idn, out):
    with ExitStack() as ctx:
        def sb(name, shape, dt=F32):
            return ctx.enter_context(nc.sbuf_tensor(name, shape, dt))

        def sem(name):
            return ctx.enter_context(nc.semaphore(name))

        w1_s = sb("w1_hi", [P, HC, F], F32R), sb("w1_lo", [P, HC, F], F32R)
        w2_s = sb("w2_hi", [P, FB, N], F32R), sb("w2_lo", [P, FB, N], F32R)
        pw = sb("pw", [P, HC])
        b1c = sb("b1c", [P, FB])
        b2_row = sb("b2_row", [P, N])
        w1_in = w1.rearrange("(c p) m -> p c m", p=P)
        w2_in = w2.rearrange("(f p) m -> p f m", p=P)
        w1_raw = sb("w1_raw", [P, RING, HC, GROUP * P])
        w2_raw = sb("w2_raw", [P, RING, GROUP, N])
        consts_loaded, raw_loaded = sem("consts_loaded"), [sem(f"w_raw_loaded{i}") for i in range(RING)]
        w_hi, w_lo = sem("w_hi"), sem("w_lo")

        mid = sb("mid", [P, TT, N])
        res = sb("res", [P, TT, N])
        hT = sb("hTn_hi", [P, HC, N], F32R), sb("hTn_lo", [P, HC, N], F32R)
        g = sb("g", [P, 2, N])
        g_s = sb("g_hi", [P, 2, N], F32R), sb("g_lo", [P, 2, N], F32R)
        ps = [ctx.enter_context(nc.psum_tensor(f"b_bank{i}", [P, N], F32)) for i in range(8)]
        bank_d, bank_o = ps[0:4], ps[4:8]

        mean, root, inverse = sem("mean"), sem("root"), sem("inverse")
        mid_loaded, res_loaded, res_ready, stored = sem("mid_loaded"), sem("res_loaded"), sem("res_ready"), sem("stored")
        normed, turned, turn_hi, turn_lo = sem("normed"), sem("turned"), sem("turn_hi"), sem("turn_lo")
        up_filled, gelu_done, g_rounded, g_ready = sem("up_filled"), sem("gelu_done"), sem("g_rounded"), sem("g_ready")
        down_done, out_filled, out_ready = sem("down_done"), sem("out_filled"), sem("out_ready")
        SPLIT3 = ((0, 0), (1, 0), (0, 1))

        def tokens(a, t):
            return a.rearrange("(t j p) n -> t p j n", p=P, j=TT)[t]

        block = ctx.enter_context(nc.Block())

        @block.sync
        def _(sp):
            def tile(t, more):
                after(sp, stored, t * 16)
                sp.dma_start(res[:], tokens(lat_dram, t)).then_inc(res_loaded, 16)
                if more:
                    sp.wait_ge(turned, t * TT + TT)
                    sp.dma_start(mid[:], tokens(mid_dram, t + 1)).then_inc(mid_loaded, 16)
                sp.wait_ge(out_ready, t * TT + TT)
                sp.dma_start(tokens(out, t), res[:]).then_inc(stored, 16)

            def weights(i):
                if i >= RING:
                    sp.wait_ge(w_lo, i - RING + 1)
                group = slice(i * GROUP, i * GROUP + GROUP)
                sp.dma_start(w1_raw[:, i % RING], w1_in[:, :, i * GROUP * P:(i + 1) * GROUP * P]
                             ).then_inc(raw_loaded[i % RING], 16)
                sp.dma_start(w2_raw[:, i % RING], w2_in[:, group, :]).then_inc(raw_loaded[i % RING], 16)

            for dst, src in ((pw[:], post_w), (b1c[:], b1), (b2_row[:], b2.partition_broadcast(P))):
                sp.dma_start(dst, src).then_inc(consts_loaded, 16)
            sp.dma_start(mid[:], tokens(mid_dram, 0)).then_inc(mid_loaded, 16)
            for i in range(GROUPS):
                weights(i)
            tile(0, True)
            with sp.Fori(1, TILES - 1) as t:
                tile(t, True)
            tile(TILES - 1, False)
            sp.wait_ge(stored, 16 * TILES)

        @block.tensor
        def _(pe):
            def turn(t, first=False):
                pe.wait_ge(normed, t * TT + TT)
                for j in range(TT):
                    if not first:
                        pe.wait_ge(gelu_done, t * FB - TT + j + 1)
                    for hc in range(HC):
                        mm = pe.transpose(bank_d[j][:, hc * P:(hc + 1) * P], mid[:, j, hc * P:(hc + 1) * P], idn[:])
                    mm.then_inc(turned, 1)

            def up(t, f):
                if f == 0:
                    pe.wait_ge(turn_lo, t * TT + TT)
                if f >= TT:
                    pe.wait_ge(gelu_done, t * FB + f - TT + 1)
                if isinstance(t, int) and t == 0 and f % GROUP == 0:
                    pe.wait_ge(w_lo, f // GROUP + 1)
                for i, (wp, mp) in enumerate(SPLIT3):
                    for hc in range(HC):
                        mm = pe.matmul(bank_d[f % 4][:, :], w1_s[wp][:, hc, f * P:(f + 1) * P], hT[mp][:, hc, :],
                                       start=(i == 0 and hc == 0), stop=(i == 2 and hc == HC - 1))
                mm.then_inc(up_filled, 1)

            def down(t, f):
                pe.wait_ge(g_ready, t * FB + f + 1)
                if f == 0:
                    after(pe, out_ready, t * TT)
                for j in range(TT):
                    for i, (gp, wp) in enumerate(SPLIT3):
                        mm = pe.matmul(bank_o[j][:, :], g_s[gp][:, f % 2, j * P:(j + 1) * P], w2_s[wp][:, f, :],
                                       start=(f == 0 and i == 0), stop=(f == FB - 1 and i == 2))
                    if f == FB - 1:
                        mm.then_inc(out_filled, 1)
                    elif j == TT - 1:
                        mm.then_inc(down_done, 1)

            def tile(t, more):
                for f in range(FB):
                    up(t, f)
                    if f == FB - 1 and more:
                        turn(t + 1)
                    if f:
                        down(t, f - 1)
                down(t, FB - 1)

            turn(0, first=True)
            tile(0, True)
            with pe.Fori(1, TILES - 1) as t:
                tile(t, True)
            tile(TILES - 1, False)

        @block.scalar
        def _(act):
            act.wait_ge(mean, 1)
            act.activation(rms[:], ssq[:], ACT.Sqrt).then_inc(root, 1)

            def turn_round(t):
                for j in range(TT):
                    act.wait_ge(turned, t * TT + j + 1)
                    act.activation(hT[0][:, :, j * P:(j + 1) * P], bank_d[j][:, :].rearrange("p (c t) -> p c t", c=HC),
                                   ACT.Copy).then_inc(turn_hi, 1)

            def tile(t, more):
                for f in range(FB):
                    act.wait_ge(up_filled, t * FB + f + 1)
                    after(act, g_ready, t * FB + max(f - 1, 0))
                    act.activation(g[:, f % 2, :], bank_d[f % 4][:, :], ACT.Gelu_apprx_tanh,
                                   bias=b1c[:, f:f + 1]).then_inc(gelu_done, 1)
                    if isinstance(t, int) and t == 0 and f % GROUP == 1 and f // GROUP + 2 < GROUPS:
                        weights(f // GROUP + 2)
                if more:
                    turn_round(t + 1)

            def weights(i):
                act.wait_ge(raw_loaded[i % RING], 32 * (i // RING + 1))
                for c in range(HC):
                    act.activation(w1_s[0][:, c, i * GROUP * P:(i + 1) * GROUP * P], w1_raw[:, i % RING, c, :],
                                   ACT.Identity, scale=pw[:, c:c + 1])
                act.activation(w2_s[0][:, i * GROUP:(i + 1) * GROUP, :], w2_raw[:, i % RING], ACT.Copy).then_inc(w_hi, 1)

            act.wait_ge(consts_loaded, 48)
            weights(0)
            turn_round(0)
            weights(1)
            tile(0, True)
            with act.Fori(1, TILES - 1) as t:
                tile(t, True)
            tile(TILES - 1, False)

        @block.vector
        def _(dve):
            dve.tensor_scalar(ssq[:], ssq[:], 1.0 / N, EPS, ALU.mult, ALU.add).then_inc(mean, 1)
            dve.wait_ge(root, 1)
            dve.reciprocal(rms[:], rms[:]).then_inc(inverse, 1)
            dve.wait_ge(inverse, 1)

            def norm(t):
                dve.wait_ge(mid_loaded, t * 16 + 16)
                for j in range(TT):
                    dve.tensor_scalar(mid[:, j, :], mid[:, j, :], rms[:, bass.ds(t * TT + j, 1)], None,
                                      ALU.mult).then_inc(normed, 1)

            def turn_rest(t):
                for j in range(TT):
                    dve.wait_ge(turn_hi, t * TT + j + 1)
                    dve.tensor_tensor(hT[1][:, :, j * P:(j + 1) * P], bank_d[j][:, :].rearrange("p (c t) -> p c t", c=HC),
                                      hT[0][:, :, j * P:(j + 1) * P].bitcast(F32), ALU.subtract).then_inc(turn_lo, 1)

            def split(t, f):
                dve.wait_ge(gelu_done, t * FB + f + 1)
                if f >= 2:
                    dve.wait_ge(down_done, t * (FB - 1) + f - 1)
                else:
                    after(dve, out_filled, t * TT)
                dve.tensor_copy(g_s[0][:, f % 2, :], g[:, f % 2, :]).then_inc(g_rounded, 1)
                dve.wait_ge(g_rounded, t * FB + f + 1)
                dve.tensor_tensor(g_s[1][:, f % 2, :], g[:, f % 2, :], g_s[0][:, f % 2, :].bitcast(F32),
                                  ALU.subtract).then_inc(g_ready, 1)

            def tile(t, more):
                for f in range(FB):
                    split(t, f)
                    if f == FB // 2 and more:
                        norm(t + 1)
                    if isinstance(t, int) and t == 0 and f % GROUP == 1 and f // GROUP + 2 < GROUPS:
                        weights(f // GROUP + 2)
                if more:
                    turn_rest(t + 1)
                dve.wait_ge(res_ready, t + 1)
                for j in range(TT):
                    dve.wait_ge(out_filled, t * TT + j + 1)
                    dve.tensor_tensor(res[:, j, :], bank_o[j][:, :], res[:, j, :], ALU.add).then_inc(out_ready, 1)

            def weights(i):
                dve.wait_ge(w_hi, i + 1)
                for c in range(HC):
                    part = slice(i * GROUP * P, (i + 1) * GROUP * P)
                    dve.scalar_tensor_tensor(out=w1_s[1][:, c, part], in0=w1_raw[:, i % RING, c, :],
                                             scalar=pw[:, c:c + 1], in1=w1_s[0][:, c, part].bitcast(F32),
                                             op0=ALU.mult, op1=ALU.subtract)
                part = slice(i * GROUP, (i + 1) * GROUP)
                dve.tensor_tensor(w2_s[1][:, part, :], w2_raw[:, i % RING], w2_s[0][:, part, :].bitcast(F32),
                                  ALU.subtract).then_inc(w_lo, 1)

            norm(0)
            dve.wait_ge(consts_loaded, 48)
            weights(0)
            turn_rest(0)
            weights(1)
            tile(0, True)
            with dve.Fori(1, TILES - 1) as t:
                tile(t, True)
            tile(TILES - 1, False)

        @block.gpsimd
        def _(pool):
            with pool.Fori(0, TILES) as t:
                pool.wait_ge(res_loaded, t * 16 + 16)
                for j in range(TT):
                    ins = pool.tensor_tensor(res[:, j, :], res[:, j, :], b2_row[:, :], ALU.add)
                ins.then_inc(res_ready, 1)


def kernel(x, ctx_2048, mask_BxS2_ik0, L0_xattn_Wq, L0_xattn_bq, L0_xattn_Wk, L0_xattn_bk, L0_xattn_Wv,
           L0_xattn_bv, L1_xattn_q_w, L1_xattn_q_b, L1_xattn_kv_w, L1_xattn_kv_b, L1_xattn_out_w,
           L1_xattn_out_b, L1_xattn_postnorm_w, L1_xattn_mlp_w1, L1_xattn_mlp_b1, L1_xattn_mlp_w2,
           L1_xattn_mlp_b2):
    import concourse.bacc as bacc
    from concourse.bass_utils import run_bass_kernel_spmd

    def stacked(a):
        return np.tile(np.asarray(a).T, (1, 3))

    def by_quarter(a):
        a = np.asarray(a)
        a = a.reshape(*a.shape[:-1], QUARTERS, HQ, D, 2)
        return np.moveaxis(a, -1, -3).reshape(*a.shape[:-4], 2 * N)

    def columns(a, n):
        return np.asarray(a).reshape(n, P).T

    arrays = dict(
        x=x, ctx_in=ctx_2048, mask=np.asarray(mask_BxS2_ik0).reshape(B, QB, P).transpose(0, 2, 1),
        wq3=stacked(L0_xattn_Wq), bq3=np.tile(np.asarray(L0_xattn_bq), 3).reshape(3 * D, 1),
        wk3=stacked(L0_xattn_Wk), bk3=np.tile(np.asarray(L0_xattn_bk), 3).reshape(3 * D, 1),
        wvT=np.asarray(L0_xattn_Wv).T, bv=columns(L0_xattn_bv, QB),
        q_w=L1_xattn_q_w, q_b=L1_xattn_q_b, kv_w=by_quarter(L1_xattn_kv_w), kv_b=by_quarter(L1_xattn_kv_b),
        out_w=L1_xattn_out_w, out_b=L1_xattn_out_b, post_w=columns(L1_xattn_postnorm_w, HC),
        w1=L1_xattn_mlp_w1, b1=columns(L1_xattn_mlp_b1, FB), w2=L1_xattn_mlp_w2, b2=L1_xattn_mlp_b2,
        ident=np.eye(P, dtype=np.float32))
    arrays = {f"in_{k}": np.ascontiguousarray(v) for k, v in arrays.items()}
    nc = bacc.Bacc("TRN2", target_bir_lowering=False, num_devices=1)
    args = [nc.dram_tensor(k, v.shape, mybir.dt.from_np(v.dtype), kind="ExternalInput").ap() for k, v in arrays.items()]
    result = nc.dram_tensor("result", (B * C, N), F32, kind="ExternalOutput").ap()
    build(nc, *args, result)
    r = run_bass_kernel_spmd(nc, [arrays], core_ids=[0])
    return r.results[0]["result"].reshape(B, C, N)
```
